# Optimizing a Trainium2 kernel written in Bass

```python
import numpy as np
import jax
import jax.numpy as jnp

def _softmax(x, axis=-1):
    return jax.nn.softmax(x, axis=axis)

def _gelu(x):
    return jax.nn.gelu(x, approximate=True)

def _silu(x):
    return jax.nn.silu(x)

def _sigmoid(x):
    return jax.nn.sigmoid(x)

def _layernorm(x, axis=-1, eps=1e-05):
    m = jnp.mean(x, axis=axis, keepdims=True)
    v = jnp.var(x, axis=axis, keepdims=True)
    return (x - m) / jnp.sqrt(v + eps)

def _scatter_add(tgt, idx, src, axis=0):
    return tgt.at[idx].add(src)

def _segment_sum(src, seg, n):
    return jax.ops.segment_sum(src, seg, n)
kernel_name = 'mk_xattn_ffn_d1_seqx_r4_3042fd'

def setup_inputs(seed: int=0):
    np.random.seed(seed)
    _w = jnp.asarray

    def _rec_inputs():
        import jax
        import jax.numpy as jnp
        _rk = jax.random.key(seed)
        x = -7.109e-05 + 0.9999 * jax.random.normal(jax.random.fold_in(_rk, 1), (4, 512, 512), jnp.float32)
        _lenS = 512 - jax.random.randint(jax.random.fold_in(_rk, 7), (4,), 0, max(1, 512 // 4) + 1, jnp.int32)
        _lenS2 = 512 - jax.random.randint(jax.random.fold_in(_rk, 8), (4,), 0, max(1, 512 // 4) + 1, jnp.int32)
        _ctx_2048P = jax.random.normal(jax.random.fold_in(_rk, 11), (4, 16, 512), jnp.float32)
        _ctx_2048c = jax.random.dirichlet(jax.random.fold_in(_rk, 511), 0.3 * jnp.ones((16,), jnp.float32), (4, 512))
        _ctx_2048t = jnp.einsum('bsk,bkd->bsd', _ctx_2048c, _ctx_2048P)
        _ctx_2048t = _ctx_2048t * jax.lax.rsqrt(jnp.mean(jnp.square(_ctx_2048t)) + 1e-12) * 0.953939
        ctx_2048 = -3.05549e-07 + 0.0199987 * (_ctx_2048t + 0.3 * jax.random.normal(jax.random.fold_in(_rk, 611), (4, 512, 512), jnp.float32))
        return (x, ctx_2048)
    x, ctx_2048 = _rec_inputs()

    def _L0_xattn_setup():
        import jax, jax.numpy as jnp
        import numpy as np
        FP8_MAX = 448.0
        ACT_EPS = 0.0001
        W_EPS = 1e-06
        BLK = 128

        def quant_dequant_act_1x128(x):
            E, M, K = x.shape
            xb = x.reshape(E, M, K // BLK, BLK)
            amax = jnp.max(jnp.abs(xb), axis=-1, keepdims=True)
            safe = jnp.maximum(amax, ACT_EPS)
            q = (xb * (FP8_MAX / safe)).astype(jnp.float8_e4m3fn)
            return (q.astype(jnp.float32) * (safe / FP8_MAX)).reshape(E, M, K)

        def quant_dequant_weight_128x128(w):
            E, N, K = w.shape
            wb = w.reshape(E, N // BLK, BLK, K // BLK, BLK)
            amax = jnp.max(jnp.abs(wb), axis=(2, 4), keepdims=True)
            safe = jnp.maximum(amax, W_EPS)
            q = (wb * (FP8_MAX / safe)).astype(jnp.float8_e4m3fn)
            return (q.astype(jnp.float32) * (safe / FP8_MAX)).reshape(E, N, K)
        key = jax.random.key(seed)
        kx, kw = jax.random.split(key)
        E, M, K, N = (8, 1024, 512, 512)
        x = jax.random.normal(kx, (E, M, K), dtype=jnp.float32)
        weight = jax.random.normal(kw, (E, N, K), dtype=jnp.float32) * 0.02
        return {'x': x, 'weight': weight}
    _L0_xattn_all = _L0_xattn_setup()
    _L0_xattn_in = {k: v for k, v in _L0_xattn_all.items() if k in ()}
    del _L0_xattn_all

    def _L0_ffn_setup():
        import jax, jax.numpy as jnp
        import numpy as np
        B, T, D = (4, 512, 512)
        E = 8
        K = 2
        F = 2048 // (E // 2)
        key = jax.random.key(seed)
        ks = jax.random.split(key, 5)
        s_in = 1.0 / np.sqrt(D)
        s_mid = 1.0 / np.sqrt(F)
        x = jax.random.normal(ks[0], (B, T, D), dtype=jnp.float32)
        Wr = jax.random.normal(ks[1], (D, E), dtype=jnp.float32) * s_in
        Wg = jax.random.normal(ks[2], (E, D, F), dtype=jnp.float32) * s_in
        Wu = jax.random.normal(ks[3], (E, D, F), dtype=jnp.float32) * s_in
        Wd = jax.random.normal(ks[4], (E, F, D), dtype=jnp.float32) * s_mid
        return {'x': x, 'Wr': Wr, 'Wg': Wg, 'Wu': Wu, 'Wd': Wd}
    _L0_ffn_all = _L0_ffn_setup()
    _L0_ffn_in = {k: v for k, v in _L0_ffn_all.items() if k in ('Wr', 'Wg', 'Wu', 'Wd')}
    del _L0_ffn_all
    return {'x': x, 'ctx_2048': ctx_2048, 'L0_ffn_Wr': _L0_ffn_in['Wr'], 'L0_ffn_Wg': _L0_ffn_in['Wg'], 'L0_ffn_Wu': _L0_ffn_in['Wu'], 'L0_ffn_Wd': _L0_ffn_in['Wd']}

def reference(x, ctx_2048, L0_ffn_Wr, L0_ffn_Wg, L0_ffn_Wu, L0_ffn_Wd):
    import jax
    import jax.numpy as jnp

    def _L0_xattn_ref(x, weight):
        import jax, jax.numpy as jnp
        import numpy as np
        FP8_MAX = 448.0
        ACT_EPS = 0.0001
        W_EPS = 1e-06
        BLK = 128

        def quant_dequant_act_1x128(x):
            E, M, K = x.shape
            xb = x.reshape(E, M, K // BLK, BLK)
            amax = jnp.max(jnp.abs(xb), axis=-1, keepdims=True)
            safe = jnp.maximum(amax, ACT_EPS)
            q = (xb * (FP8_MAX / safe)).astype(jnp.float8_e4m3fn)
            return (q.astype(jnp.float32) * (safe / FP8_MAX)).reshape(E, M, K)

        def quant_dequant_weight_128x128(w):
            E, N, K = w.shape
            wb = w.reshape(E, N // BLK, BLK, K // BLK, BLK)
            amax = jnp.max(jnp.abs(wb), axis=(2, 4), keepdims=True)
            safe = jnp.maximum(amax, W_EPS)
            q = (wb * (FP8_MAX / safe)).astype(jnp.float8_e4m3fn)
            return (q.astype(jnp.float32) * (safe / FP8_MAX)).reshape(E, N, K)
        xq = quant_dequant_act_1x128(x)
        wq = quant_dequant_weight_128x128(weight)
        return jnp.einsum('emk,enk->emn', xq, wq)

    def _L0_ffn_ref(x, Wr, Wg, Wu, Wd):
        import jax, jax.numpy as jnp
        import numpy as np
        B, T, D = (4, 512, 512)
        E = 8
        K = 2
        F = 2048 // (E // 2)
        probs = jax.nn.softmax(x @ Wr, axis=-1)
        topk_w, topk_idx = jax.lax.top_k(probs, K)
        topk_w = topk_w / jnp.sum(topk_w, axis=-1, keepdims=True)
        output = jnp.zeros_like(x)
        for i in range(E):
            sel = topk_idx == i
            w_i = jnp.sum(topk_w * sel.astype(x.dtype), axis=-1, keepdims=True)
            h = jax.nn.silu(x @ Wg[i]) * (x @ Wu[i])
            e_out = h @ Wd[i]
            output = output + w_i * e_out
        return output
    x = x + _L0_xattn_ref(_layernorm(x, axis=-1), ctx_2048)
    x = x + _L0_ffn_ref(_layernorm(x, axis=-1), L0_ffn_Wr, L0_ffn_Wg, L0_ffn_Wu, L0_ffn_Wd)
    return x

_drawn_inputs = setup_inputs


def setup_inputs(seed=0):
    import zlib

    import numpy as np

    out = dict(_drawn_inputs(seed))
    spreads = {}
    factors = {}
    for name, (base, spread) in spreads.items():
        noise = np.random.default_rng([zlib.crc32(name.encode()), seed]).standard_normal(out[name].shape)
        drawn = base * np.exp(spread * noise) if base else spread * noise
        out[name] = jnp.asarray(drawn.astype(out[name].dtype))
    for name, factor in factors.items():
        out[name] = (out[name] * factor).astype(out[name].dtype)
    return out
```

```python
from contextlib import ExitStack

import concourse.bass as bass
from concourse import mybir

F32 = mybir.dt.float32
F32R = mybir.dt.float32r
BF16 = mybir.dt.bfloat16
I32 = mybir.dt.int32
U32 = mybir.dt.uint32
ALU = mybir.AluOpType
ACT = mybir.ActivationFunctionType
AX_X = mybir.AxisListType.X
ds = bass.ds

P = 128
B, S, D = 4, 512, 512
E, F, TOPK = 8, 512, 2
KC = D // P
TB = S // P
NT = B * TB
LN_EPS = 1e-5
FP8_MAX, ACT_EPS, W_EPS = 448.0, 1e-4, 1e-6

CAP = B * S + P
ZROW = E * CAP
NTILE = (TOPK * B * S + E * (P - 1)) // P
T_PAR, T_WREADY, T_ROW, T_PAD, T_FREE, T_END = 0, 40, 80, 120, 128, 136

EXP_MASK = 0x7F800000
MIN_NORMAL = 2.0 ** -6
ROUND_AT = 1.5 * 2.0 ** 20


class Chain:

    def __init__(self, eng, sem, per, i):
        self.eng, self.sem, self.per, self.start, self.n = eng, sem, per, i * per, 0

    def add(self, ins):
        ins.then_inc(self.sem, 1)
        self.n += 1

    def sync(self):
        self.eng.wait_ge(self.sem, self.start + self.n)

    def sync_alone(self, wait_alone):
        wait_alone(self.eng, self.sem, self.start + self.n)

    def link(self, ins):
        self.add(ins)
        self.sync()

    def close(self):
        assert self.n == self.per, (self.n, self.per)


def xattn_moe(nc, x, ctx_in, Wr, Wg, Wu, Wd, out):
    with ExitStack() as ctx:
        def sb(name, shape, dt):
            return ctx.enter_context(nc.sbuf_tensor(name, shape, dt))

        def sem(name):
            return ctx.enter_context(nc.semaphore(name))

        x1 = sb("x1", [P, NT, D], F32)
        wsplit = sb("wsplit", [P, 2, 3, 2, KC, F], F32R)
        wraw = sb("wraw", [P, 2, KC, F], F32)
        ctxq = sb("ctxq", [P, TB, D], F32)
        xq = sb("xq", [P, TB, D], F32)
        magx = sb("magx", [P, 2, 2 * D], F32)
        magc = sb("magc", [P, 2, 2 * D], F32)
        y2 = sb("y2", [P, TB, D], F32)
        y2T = sb("y2T", [P, KC, P], F32)
        xT = sb("xT", [P, 2, 2, KC, P], F32R)
        hT = sb("hT", [P, 2, KC, P], F32R)
        wr = sb("wr", [P, KC, E], F32)
        ident = sb("ident", [P, P], F32)
        before = sb("before", [P, P], BF16)
        ones = sb("ones", [P, P], BF16)
        iot = sb("iot", [P, 64], I32)
        alti = sb("alti", [P, E], I32)
        io = sb("io", [P, 64], F32)
        alt = sb("alt", [P, E], F32)
        rev = sb("rev", [P, E], F32)
        cape = sb("cape", [P, E], F32)
        eps = sb("eps", [P, 1], F32)
        stats = sb("stats", [P, 2, TB, 6], F32)
        mv = sb("mv", [P, 2, TB, 2], F32)
        sd = sb("sd", [P, 2, TB], F32)
        rstd = sb("rstd", [P, 2, TB], F32)
        nmr = sb("nmr", [P, 2, TB], F32)
        NB = TB * KC
        xmax = sb("xmax", [P, NB], F32)
        xsc = sb("xsc", [P, NB], F32)
        xinv = sb("xinv", [P, NB], F32)
        cmaxp = sb("cmaxp", [P, NB], F32)
        cmax = sb("cmax", [P, NB], F32)
        csc = sb("csc", [P, NB], F32)
        cinv = sb("cinv", [P, NB], F32)
        rl = sb("rl", [P, TB, E], F32)
        rl2 = sb("rl2", [P, TB, E], F32)
        eq = sb("eq", [P, TB, E], F32)
        top = sb("top", [P, 2, TB], F32)
        pick = sb("pick", [P, 2, TB], F32)
        oh = sb("oh", [P, 2, TB, E], F32)
        selb = sb("selb", [P, TB, E], BF16)
        cum = sb("cum", [P, TB + 1, E], BF16)
        place = sb("place", [P, TB, E], F32)
        slot = sb("slot", [P, TB, 2], F32)
        slot_i = sb("slot_i", [P, TB, 2], I32)
        oh_all = sb("oh_all", [P, 2, NT, E], F32)
        slot_all = sb("slot_all", [P, NT, 2], F32)
        lg_all = sb("lg_all", [P, NT, E], F32)
        m_all = sb("m_all", [P, NT], F32)
        yrow_i = sb("yrow_i", [P, NT, 2], I32)
        wmix = sb("wmix", [P, 2, NT], F32)
        count = sb("count", [P, 4, E], F32)
        tabf = sb("tabf", [P, T_END], F32)
        tab = sb("tab", [P, T_END], I32)
        small = sb("small", [P, 4, NT], F32)

        cT = wsplit[:, 1, 0, :, :, :]
        rows = magx[:, 0, 0:D]
        hid = magx[:, 1, 0:F]
        sg = magx[:, 1, F:2 * F]
        yt = magc[:, 0, 0:D]
        zero = magc[:, 0, D:2 * D]
        le = magc[:, 1, 0:NTILE * E].rearrange("p (t e) -> p t e", e=E)
        le2 = magc[:, 1, 512:512 + NTILE * E].rearrange("p (t e) -> p t e", e=E)
        over = y2T[:, 0, :].rearrange("p (e j) -> p e j", j=NT)
        ohm = y2T[:, 0:2, :].rearrange("p k c -> p (k c)").rearrange("p (a t e) -> p (a t) e", a=2, e=E)
        expo = y2T[:, 2, :].rearrange("p (t e) -> p t e", e=E)
        expo2 = y2T[:, 3, :].rearrange("p (t e) -> p t e", e=E)

        ps = [ctx.enter_context(nc.psum_tensor(f"ps{i}", [P, 512], F32)) for i in range(8)]
        ps_cT, ps_xT, ps_at, ps_yT, ps_small = ps[0:2], ps[2:4], ps[4:6], ps[6], ps[7]
        ps_g, ps_u, ps_y, ps_hT, ps_rT = ps[0], ps[1], ps[4], ps[5], ps[2]

        grouped = nc.dram_tensor("grouped", [ZROW + P, D], F32, kind="Internal").ap()
        results = nc.dram_tensor("results", [NTILE * P, D], F32, kind="Internal").ap()

        x_rows = x.rearrange("b s d -> (b s) d")
        out_rows = out.rearrange("b s d -> (b s) d")
        weights = (Wg, Wu, Wd)

        x_loaded, ctx_loaded, wr_loaded = sem("x_loaded"), sem("ctx_loaded"), sem("wr_loaded")
        masks_ready, consts_ready, pool_set = sem("masks_ready"), sem("consts_ready"), sem("pool_set")
        dve_const = sem("dve_const")
        ctx_maxed, ctx_max_all = sem("ctx_maxed"), sem("ctx_max_all")
        ln1_var, ln1_sd, ln1_ready, ln1_done = sem("ln1_var"), sem("ln1_sd"), sem("ln1_ready"), sem("ln1_done")
        ctx_biased, ctx_rounded, ctx_ready = sem("ctx_biased"), sem("ctx_rounded"), sem("ctx_ready")
        x_biased, x_rounded, xq_ready = sem("x_biased"), sem("x_rounded"), sem("xq_ready")
        cT_formed, cT_high, cT_low = sem("cT_formed"), sem("cT_high"), sem("cT_low")
        xT_formed, xT_high, xT_low = sem("xT_formed"), sem("xT_high"), sem("xT_low")
        attn_done, x1_ready = sem("attn_done"), sem("x1_ready")
        ln2_var, ln2_sd, ln2_ready, y2_ready = sem("ln2_var"), sem("ln2_sd"), sem("ln2_ready"), sem("y2_ready")
        yT_formed, yT_ready, logits_done = sem("yT_formed"), sem("yT_ready"), sem("logits_done")
        chosen, ranks_done, slots_ready = sem("chosen"), sem("ranks_done"), sem("slots_ready")
        scattered = sem("scattered")
        w_loaded = [sem("w_loaded0"), sem("w_loaded1")]
        w_split, w_ready = sem("w_split"), sem("w_ready")
        counts_done, table_ready, zero_ready = sem("counts_done"), sem("table_ready"), sem("zero_ready")
        padded, rows_loaded = sem("padded"), sem("rows_loaded")
        rT_formed, rT_high, rT_low = sem("rT_formed"), sem("rT_high"), sem("rT_low")
        up_done, silu_done, hid_ready = sem("up_done"), sem("silu_done"), sem("hid_ready")
        hT_formed, hT_high, hT_low = sem("hT_formed"), sem("hT_high"), sem("hT_low")
        tiles_done, yt_ready, yt_stored = sem("tiles_done"), sem("yt_ready"), sem("yt_stored")
        exp_in, exp_done, mix_ready = sem("exp_in"), sem("exp_done"), sem("mix_ready")
        fetched = [sem(f"fetched{s}") for s in range(TB)]
        mixed, row_ready, out_stored = sem("mixed"), sem("row_ready"), sem("out_stored")
        waited = sem("waited")
        dve_q, dve_a, dve_r, dve_t, dve_m = (sem(n) for n in ("dve_q", "dve_a", "dve_r", "dve_t", "dve_m"))

        def wait_alone(eng, sem_, value):
            eng.wait_ge(sem_, value)
            eng.sem_inc(waited, 1)

        block = ctx.enter_context(nc.Block())

        @block.sync
        def _(sp):
            def load_x(b):
                sp.dma_start(x1[:, TB * b:TB * b + TB, :],
                             x_rows[S * b:S * b + S, :].rearrange("(t p) d -> p t d", p=P)).then_inc(x_loaded, 16)

            def load_ctx(b):
                sp.dma_start(ctxq[:, :, :], ctx_in[b].rearrange("(t p) d -> p t d", p=P)).then_inc(ctx_loaded, 16)

            load_ctx(0)
            load_x(0)
            sp.dma_start(wr[:, :, :], Wr.rearrange("(k p) e -> p k e", p=P)).then_inc(wr_loaded, 16)
            for b in range(1, B):
                sp.wait_ge(x_loaded, 16 * b)
                load_x(b)
            for b in range(1, B):
                sp.wait_ge(cT_formed, TB * b)
                load_ctx(b)

            sp.wait_ge(zero_ready, 1)
            sp.dma_start(grouped[ZROW:ZROW + P, :], zero).then_inc(padded, 16)
            sp.wait_ge(table_ready, 1)
            for e in range(E):
                pad = sp.value_load(tab[0:1, T_PAD + e:T_PAD + e + 1], min_val=0, max_val=ZROW - P)
                sp.dma_start(grouped[ds(pad, P), :], zero).then_inc(padded, 16)
            sp.wait_ge(padded, 16 * (E + 1))
            sp.wait_ge(scattered, 16 * 2 * NT)

            def load_rows(t):
                row = sp.value_load(tab[0:1, ds(T_ROW + t, 1)], min_val=0, max_val=ZROW)
                sp.dma_start(rows, grouped[ds(row, P), :]).then_inc(rows_loaded, 16)

            def store_result(t):
                sp.wait_ge(yt_ready, t + 1)
                sp.dma_start(results[ds(t * P, P), :], yt).then_inc(yt_stored, 16)

            load_rows(0)
            sp.wait_ge(rT_formed, 1)
            load_rows(1)
            sp.wait_ge(rT_formed, 2)
            load_rows(2)
            with sp.Fori(1, NTILE - 2) as t:
                sp.wait_ge(rT_formed, t + 2)
                load_rows(t + 2)
                store_result(t - 1)
            for t in range(NTILE - 3, NTILE):
                store_result(t)

            with sp.Fori(0, NT) as i:
                sp.wait_ge(row_ready, i + 1)
                sp.dma_start(out_rows[ds(i * P, P), :],
                             x1[:, ds(i, 1), :].rearrange("p a d -> p (a d)")).then_inc(out_stored, 16)
            sp.wait_ge(out_stored, 16 * NT)

        @block.gpsimd
        def _(pool):
            nc.gpsimd.memset(ident[:, :], 0.0).then_inc(pool_set, 1)
            nc.gpsimd.memset(before[:, :], 1.0).then_inc(pool_set, 1)
            nc.gpsimd.memset(ones[:, :], 1.0).then_inc(pool_set, 1)
            nc.gpsimd.iota(iot[:, :], pattern=[[1, 64]], base=0, channel_multiplier=0).then_inc(pool_set, 1)
            nc.gpsimd.iota(alti[:, :], pattern=[[0, E // 2], [-2, 2]], base=1, channel_multiplier=0).then_inc(pool_set, 1)
            pool.wait_ge(pool_set, 5)
            nc.gpsimd.affine_select(out=ident[:, :], in_=ident[:, :], compare_op=ALU.not_equal, fill=1.0,
                                    base=0, pattern=[[-1, P]], channel_multiplier=1).then_inc(masks_ready, 1)
            nc.gpsimd.affine_select(out=before[:, :], in_=before[:, :], compare_op=ALU.is_gt, fill=0.0,
                                    base=0, pattern=[[1, P]], channel_multiplier=-1).then_inc(masks_ready, 1)

            def load_weights(e, m, stage):
                src = weights[m][ds(e, 1)].rearrange("a (k p) f -> p (a k) f", p=P)
                pool.dma_start(wraw[:, stage, :, :], src).then_inc(w_loaded[stage], 16)

            def split_weights(m, slot_, stage, nth, count_before, last):
                wait_alone(pool, w_loaded[stage], 16 * (nth + 1))
                high, low = wsplit[:, slot_, m, 0, :, :], wsplit[:, slot_, m, 1, :, :]
                nc.gpsimd.tensor_copy(high, wraw[:, stage, :, :]).then_inc(w_split, 1)
                pool.wait_ge(w_split, count_before + 1)
                nc.gpsimd.tensor_tensor(low, wraw[:, stage, :, :], high.bitcast(F32),
                                        ALU.subtract).then_inc(w_split if last is None else w_ready, 1)
                if last is None:
                    wait_alone(pool, w_split, count_before + 2)
                else:
                    wait_alone(pool, w_ready, last)

            def ctx_max(b):
                wait_alone(pool, ctx_maxed, b + 1)
                nc.gpsimd.partition_all_reduce(cmax[:, :], cmaxp[:, :], P,
                                               bass.bass_isa.ReduceOp.max).then_inc(ctx_max_all, 1)

            def round_off(b):
                for h in range(2):
                    pool.wait_ge(ctx_biased, 2 * b + h + 1)
                    v = ctxq[:, 2 * h:2 * h + 2, :]
                    nc.gpsimd.tensor_tensor(v, v, magc[:, h, :].rearrange("p (t d) -> p t d", d=D),
                                            ALU.subtract).then_inc(ctx_rounded, 1)
                for h in range(2):
                    pool.wait_ge(x_biased, 2 * b + h + 1)
                    v = xq[:, 2 * h:2 * h + 2, :]
                    nc.gpsimd.tensor_tensor(v, v, magx[:, h, :].rearrange("p (t d) -> p t d", d=D),
                                            ALU.subtract).then_inc(x_rounded, 1)

            def scatter(b):
                wait_alone(pool, slots_ready, b + 1)
                for j in range(TB):
                    for c in range(2):
                        nc.gpsimd.indirect_dma_start(
                            grouped[:, :], bass.IndirectOffsetOnAxis(ap=slot_i[:, j, c:c + 1], axis=0),
                            y2[:, j, :], None).then_inc(scattered, 16)

            for m in range(2):
                load_weights(0, m, m)
            ctx_max(0)
            round_off(0)
            ctx_max(1)
            round_off(1)
            scatter(0)
            split_weights(0, 0, 0, 0, 0, None)
            load_weights(0, 2, 0)
            with pool.Fori(1, B - 1) as b:
                ctx_max(b + 1)
                round_off(b + 1)
                scatter(b)
            split_weights(1, 0, 1, 0, 2, None)
            load_weights(1, 0, 1)
            scatter(B - 1)
            split_weights(2, 0, 0, 1, 4, 1)
            load_weights(1, 1, 0)
            pool.wait_ge(attn_done, NT)
            split_weights(0, 1, 1, 1, 5, None)
            load_weights(1, 2, 1)
            split_weights(1, 1, 0, 2, 7, None)
            load_weights(2, 0, 0)
            split_weights(2, 1, 1, 2, 9, 2)
            load_weights(2, 1, 1)
            pool.wait_ge(table_ready, 1)

            def expert(e, slot_, nth0, nth1, before_, first_stage, load_next):
                free = pool.value_load(tab[0:1, ds(T_FREE + e - 2, 1)], min_val=1, max_val=NTILE + 1)
                wait_alone(pool, tiles_done, free)
                a, z = first_stage, 1 - first_stage
                n = [nth0, nth1]
                split_weights(0, slot_, a, n[a], before_, None)
                load_weights(e, 2, a)
                split_weights(1, slot_, z, n[z], before_ + 2, None)
                if load_next:
                    load_weights(e + 1, 0, z)
                split_weights(2, slot_, a, n[a] + 1, before_ + 4, e + 1)
                if load_next:
                    load_weights(e + 1, 1, a)

            with pool.Fori(0, E // 2 - 2) as q:
                expert(2 + 2 * q, 0, 3 + 3 * q, 3 + 3 * q, 10 + 10 * q, 0, True)
                expert(3 + 2 * q, 1, 5 + 3 * q, 4 + 3 * q, 15 + 10 * q, 1, True)
            expert(E - 2, 0, 9, 9, 30, 0, True)
            expert(E - 1, 1, 11, 10, 35, 1, False)

            pool.wait_ge(mix_ready, 1)
            pool.wait_ge(yt_stored, 16 * NTILE)

            def fetch(i, s):
                for c, buf in enumerate((ctxq, xq)):
                    nc.gpsimd.indirect_dma_start(
                        buf[:, s, :], None, results[:, :],
                        bass.IndirectOffsetOnAxis(ap=yrow_i[:, i, c:c + 1], axis=0)).then_inc(fetched[s], 16)

            for i in range(NT):
                if i >= TB:
                    pool.wait_ge(row_ready, i - TB + 1)
                fetch(i, i % TB)

        @block.scalar
        def _(act):
            def ln1(b):
                act.wait_ge(ln1_var, b + 1)
                nc.scalar.activation(sd[:, 0, :], mv[:, 0, :, 1], ACT.Sqrt, bias=eps[:, :]).then_inc(ln1_sd, 1)
                act.wait_ge(ln1_ready, b + 1)
                for j in range(TB):
                    xj = x1[:, ds(TB * b + j, 1), :].rearrange("p a d -> p (a d)")
                    nc.scalar.activation(xq[:, j, :], xj, ACT.Identity, bias=nmr[:, 0, j:j + 1],
                                         scale=rstd[:, 0, j:j + 1]).then_inc(ln1_done, 1)

            def dequantise(b):
                for buf, scales, rounded, ready in ((ctxq, csc, ctx_rounded, ctx_ready), (xq, xsc, x_rounded, xq_ready)):
                    for j in range(TB):
                        if j % 2 == 0:
                            act.wait_ge(rounded, 2 * b + j // 2 + 1)
                        for k in range(KC):
                            v = buf[:, j, k * P:(k + 1) * P]
                            nc.scalar.activation(v, v, ACT.Copy, scale=scales[:, KC * j + k:KC * j + k + 1]).then_inc(ready, 1)

            def attention(b):
                for k in range(KC):
                    act.wait_ge(cT_formed, KC * b + k + 1)
                    nc.scalar.activation(cT[:, 0, k, :], ps_cT[k % 2][:, :], ACT.Copy).then_inc(cT_high, 1)
                for j in range(TB):
                    act.wait_ge(xT_formed, TB * b + j + 1)
                    nc.scalar.activation(xT[:, j % 2, 0, :, :], ps_xT[j % 2][:, :].rearrange("p (k c) -> p k c", c=P),
                                         ACT.Copy).then_inc(xT_high, 1)

            def ln2(b):
                act.wait_ge(ln2_var, b + 1)
                nc.scalar.activation(sd[:, 1, :], mv[:, 1, :, 1], ACT.Sqrt, bias=eps[:, :]).then_inc(ln2_sd, 1)
                act.wait_ge(ln2_ready, b + 1)
                for j in range(TB):
                    xj = x1[:, ds(TB * b + j, 1), :].rearrange("p a d -> p (a d)")
                    nc.scalar.activation(y2[:, j, :], xj, ACT.Identity, bias=nmr[:, 1, j:j + 1],
                                         scale=rstd[:, 1, j:j + 1]).then_inc(y2_ready, 1)

            def transposed_y2(b):
                for j in range(TB):
                    act.wait_ge(yT_formed, TB * b + j + 1)
                    nc.scalar.activation(y2T[:, :, :], ps_yT[:, :].rearrange("p (k c) -> p k c", c=P),
                                         ACT.Copy).then_inc(yT_ready, 1)

            act.wait_ge(consts_ready, 1)
            ln1(0)
            dequantise(0)
            attention(0)
            ln2(0)
            ln1(1)
            transposed_y2(0)
            dequantise(1)
            with act.Fori(1, B - 1) as b:
                attention(b)
                act.wait_ge(scattered, 32 * TB * b)
                ln2(b)
                ln1(b + 1)
                transposed_y2(b)
                dequantise(b + 1)
            attention(B - 1)
            act.wait_ge(scattered, 32 * TB * (B - 1))
            ln2(B - 1)
            transposed_y2(B - 1)

            act.wait_ge(exp_in, 1)
            nc.scalar.activation(expo2, expo, ACT.Exp).then_inc(exp_done, 1)

            def high_rows(t):
                act.wait_ge(rT_formed, t + 1)
                nc.scalar.activation(xT[:, 0, 0, :, :], ps_rT[:, :].rearrange("p (k c) -> p k c", c=P),
                                     ACT.Copy).then_inc(rT_high, 1)

            def silu(t):
                act.wait_ge(up_done, 2 * t + 1)
                nc.scalar.activation(sg, ps_g[:, :], ACT.Silu).then_inc(silu_done, 1)

            def high_hid(t):
                act.wait_ge(hT_formed, t + 1)
                nc.scalar.activation(hT[:, 0, :, :], ps_hT[:, :].rearrange("p (k c) -> p k c", c=P),
                                     ACT.Copy).then_inc(hT_high, 1)

            def result(t, first=False):
                act.wait_ge(tiles_done, t + 2)
                if not first:
                    act.wait_ge(yt_stored, 16 * t)
                nc.scalar.activation(yt, ps_y[:, :], ACT.Copy).then_inc(yt_ready, 1)

            high_rows(0)
            silu(0)
            high_rows(1)
            high_hid(0)
            silu(1)
            high_rows(2)
            result(0, True)
            high_hid(1)
            with act.Fori(2, NTILE - 1) as t:
                act.wait_ge(hid_ready, t)
                silu(t)
                high_rows(t + 1)
                result(t - 1)
                high_hid(t)
            silu(NTILE - 1)
            result(NTILE - 2)
            high_hid(NTILE - 1)
            result(NTILE - 1)

        @block.vector
        def _(dve):
            V = nc.vector
            dve.wait_ge(masks_ready, 2)
            c = Chain(dve, dve_const, 7, 0)
            c.add(V.tensor_copy(io[:, :], iot[:, :]))
            c.add(V.tensor_copy(alt[:, :], alti[:, :]))
            c.add(V.memset(eps[:, :], LN_EPS))
            c.add(V.memset(cum[:, TB, :], 0.0))
            c.sync()
            c.add(V.tensor_scalar(rev[:, :], io[:, 0:E], -1.0, float(E), ALU.mult, ALU.add))
            c.add(V.tensor_scalar(cape[:, :], io[:, 0:E], float(CAP), None, ALU.mult))
            c.add(V.memset(small[:, 0, :], 0.0))
            c.close()
            c.sync()
            V.memset(small[:, 1, :], 0.0).then_inc(consts_ready, 1)

            def tiles(ap):
                return ap.unsqueeze(2).broadcast_to([P, TB, E])

            def experts(ap, n=TB):
                return ap.unsqueeze(1).broadcast_to([P, n, E])

            def blocks(ap):
                return ap.unsqueeze(2).broadcast_to([P, NB, P])

            def ln_stats(c, which, b, j):
                xj = x1[:, ds(TB * b + j, 1), :].rearrange("p a d -> p (a d)")
                c.add(V.bn_stats(stats[:, which, j, :], xj))

            def ln_scale(c, which, sd_sem, b, ready):
                dve.wait_ge(sd_sem, b + 1)
                c.link(V.reciprocal(rstd[:, which, :], sd[:, which, :]))
                V.scalar_tensor_tensor(nmr[:, which, :], mv[:, which, :, 0], -1.0, rstd[:, which, :],
                                       ALU.mult, ALU.mult).then_inc(ready, 1)

            def scales(c, maxima, scale, inv, floor):
                c.link(V.tensor_scalar(maxima[:, :], maxima[:, :], floor, None, ALU.max))
                c.add(V.tensor_scalar(scale[:, :], maxima[:, :], 1.0 / FP8_MAX, None, ALU.mult))
                c.link(V.reciprocal(inv[:, :], maxima[:, :]))
                c.link(V.tensor_scalar(inv[:, :], inv[:, :], FP8_MAX, None, ALU.mult))

            def quantise(c, buf, inv, mag, biased):
                flat = buf[:, :, :].rearrange("p t (k c) -> p (t k) c", c=P)
                c.link(V.tensor_tensor(flat, flat, blocks(inv[:, :]), ALU.mult))
                for h in range(2):
                    v = buf[:, 2 * h:2 * h + 2, :].rearrange("p t d -> p (t d)")
                    m = mag[:, h, :]
                    c.link(V.tensor_scalar(m.bitcast(U32), v.bitcast(U32), EXP_MASK, None, ALU.bitwise_and))
                    c.link(V.tensor_scalar(m, m, MIN_NORMAL, ROUND_AT, ALU.max, ALU.mult))
                    V.tensor_tensor(v, v, m, ALU.add).then_inc(biased, 1)

            def quant_first(c, b):
                dve.wait_ge(ctx_loaded, 16 * (b + 1))
                V.tensor_reduce(cmaxp[:, :], ctxq[:, :, :].rearrange("p t (k c) -> p (t k) c", c=P), AX_X, ALU.max,
                                apply_absolute_value=True).then_inc(ctx_maxed, 1)

            def quant_rest(c, b):
                wait_alone(dve, x_loaded, 16 * (b + 1))
                for j in range(TB):
                    ln_stats(c, 0, b, j)
                c.sync_alone(wait_alone)
                for j in range(TB):
                    last = V.bn_aggr(mv[:, 0, j, :], stats[:, 0, j, :])
                    if j < TB - 1:
                        c.add(last)
                last.then_inc(ln1_var, 1)
                dve.wait_ge(ctx_max_all, b + 1)
                scales(c, cmax, csc, cinv, W_EPS)
                quantise(c, ctxq, cinv, magc, ctx_biased)
                ln_scale(c, 0, ln1_sd, b, ln1_ready)
                dve.wait_ge(ln1_done, TB * (b + 1))
                c.link(V.tensor_reduce(xmax[:, :], xq[:, :, :].rearrange("p t (k c) -> p (t k) c", c=P), AX_X, ALU.max,
                                       apply_absolute_value=True))
                scales(c, xmax, xsc, xinv, ACT_EPS)
                quantise(c, xq, xinv, magx, x_biased)
                c.close()

            NQ = 4 + 3 + 4 + 5 + 1 + 1 + 4 + 5
            NA = 4 + 3 + 1

            def attention(b, b_next):
                a = Chain(dve, dve_a, NA, b)
                for k in range(KC):
                    dve.wait_ge(cT_high, KC * b + k + 1)
                    V.tensor_tensor(cT[:, 1, k, :], ps_cT[k % 2][:, :], cT[:, 0, k, :].bitcast(F32),
                                    ALU.subtract).then_inc(cT_low, 1)

                def low(j):
                    dve.wait_ge(xT_high, TB * b + j + 1)
                    V.tensor_tensor(xT[:, j % 2, 1, :, :], ps_xT[j % 2][:, :].rearrange("p (k c) -> p k c", c=P),
                                    xT[:, j % 2, 0, :, :].bitcast(F32), ALU.subtract).then_inc(xT_low, 1)

                def add(j):
                    dve.wait_ge(attn_done, TB * b + j + 1)
                    xj = x1[:, ds(TB * b + j, 1), :].rearrange("p a d -> p (a d)")
                    V.tensor_tensor(xj, ps_at[j % 2][:, :], xj, ALU.add).then_inc(x1_ready, 1)
                    wait_alone(dve, x1_ready, TB * b + j + 1)
                    ln_stats(a, 1, b, j)

                low(0)
                for j in range(1, TB):
                    low(j)
                    add(j - 1)
                add(TB - 1)
                a.sync_alone(wait_alone)
                for j in range(TB):
                    last = V.bn_aggr(mv[:, 1, j, :], stats[:, 1, j, :])
                    if j < TB - 1:
                        a.add(last)
                last.then_inc(ln2_var, 1)
                c = None
                if b_next is not None:
                    c = Chain(dve, dve_q, NQ, b_next)
                    quant_first(c, b_next)
                ln_scale(a, 1, ln2_sd, b, ln2_ready)
                a.close()
                return c

            NR = 27

            def route(b):
                r = Chain(dve, dve_r, NR, b)
                dve.wait_ge(logits_done, b + 1)
                r.add(V.tensor_copy(rl[:, :, :], ps_small[:, 0:TB * E].rearrange("p (t e) -> p t e", e=E)))
                r.add(V.tensor_copy(cum[:, 0, :], cum[:, TB, :]))
                r.sync()
                src = rl
                for n in range(2):
                    r.link(V.tensor_reduce(top[:, n, :], src[:, :, :], AX_X, ALU.max))
                    r.link(V.tensor_tensor(eq[:, :, :], src[:, :, :], tiles(top[:, n, :]), ALU.is_equal))
                    r.link(V.tensor_tensor(eq[:, :, :], eq[:, :, :], experts(rev[:, :]), ALU.mult))
                    r.link(V.tensor_reduce(pick[:, n, :], eq[:, :, :], AX_X, ALU.max))
                    r.link(V.tensor_tensor(oh[:, n, :, :], experts(rev[:, :]), tiles(pick[:, n, :]), ALU.is_equal))
                    if n == 0:
                        r.link(V.scalar_tensor_tensor(rl2[:, :, :], oh[:, 0, :, :], -3.0e38, rl[:, :, :], ALU.mult, ALU.add))
                        src = rl2
                r.link(V.tensor_tensor(selb[:, :, :], oh[:, 0, :, :], oh[:, 1, :, :], ALU.add))
                for j in range(TB):
                    last = V.tensor_tensor(cum[:, j + 1, :], cum[:, j, :], selb[:, j, :], ALU.add)
                    if j < TB - 1:
                        r.link(last)
                last.then_inc(chosen, 1)
                for n in range(2):
                    r.add(V.tensor_copy(oh_all[:, n, ds(TB * b, TB), :], oh[:, n, :, :]))
                r.add(V.tensor_copy(lg_all[:, ds(TB * b, TB), :], rl[:, :, :]))
                r.add(V.tensor_copy(m_all[:, ds(TB * b, TB)], top[:, 0, :]))
                dve.wait_ge(ranks_done, b + 1)
                r.link(V.tensor_tensor(place[:, :, :], ps_small[:, TB * E:2 * TB * E].rearrange("p (t e) -> p t e", e=E),
                                       experts(cape[:, :]), ALU.add))
                for n in range(2):
                    r.link(V.tensor_tensor(eq[:, :, :], oh[:, n, :, :], place[:, :, :], ALU.mult))
                    r.link(V.tensor_reduce(slot[:, :, n], eq[:, :, :], AX_X, ALU.add))
                r.add(V.tensor_copy(slot_all[:, ds(TB * b, TB), :], slot[:, :, :]))

                if not (isinstance(b, int) and b == 0):
                    dve.wait_ge(scattered, 32 * TB * b)
                V.tensor_copy(slot_i[:, :, :], slot[:, :, :]).then_inc(slots_ready, 1)
                r.close()

            def first_quant():
                c = Chain(dve, dve_q, NQ, 0)
                quant_first(c, 0)
                quant_rest(c, 0)

            first_quant()
            quant_rest(attention(0, 1), 1)
            route(0)
            with dve.Fori(1, B - 1) as b:
                quant_rest(attention(b, b + 1), b + 1)
                route(b)
            attention(B - 1, None)
            V.memset(zero, 0.0).then_inc(zero_ready, 1)
            route(B - 1)

            n_rows, n_tiles, upto, base = (count[:, i, :] for i in range(4))
            t = Chain(dve, dve_t, 31, 0)
            dve.wait_ge(counts_done, 1)
            t.link(V.tensor_copy(n_rows, ps_small[:, 0:E]))
            t.link(V.tensor_scalar(tabf[:, 0:NT], io[:, 0:NT], float(P), None, ALU.mult))
            t.link(V.tensor_tensor(over, n_rows.unsqueeze(2).broadcast_to([P, E, NT]),
                                   tabf[:, 0:NT].unsqueeze(1).broadcast_to([P, E, NT]), ALU.is_gt))
            t.link(V.tensor_reduce(n_tiles, over, AX_X, ALU.add))
            t.link(V.tensor_copy(upto[:, 0:1], n_tiles[:, 0:1]))
            for e in range(1, E):
                t.link(V.tensor_tensor(upto[:, e:e + 1], upto[:, e - 1:e], n_tiles[:, e:e + 1], ALU.add))
            tcol = io[:, 0:NTILE].unsqueeze(2).broadcast_to([P, NTILE, E])
            t.link(V.tensor_tensor(le, tcol, experts(upto, NTILE), ALU.is_ge))
            t.link(V.tensor_tensor(le2, le, experts(alt[:, :], NTILE), ALU.mult))
            t.link(V.tensor_reduce(tabf[:, T_PAR:T_PAR + NTILE], le2[:, :, 0:E - 1], AX_X, ALU.add))
            t.link(V.tensor_reduce(tabf[:, T_WREADY:T_WREADY + NTILE], le[:, :, 0:E - 1], AX_X, ALU.add))
            t.link(V.tensor_tensor(le2, le, experts(n_tiles, NTILE), ALU.mult))
            rowc = tabf[:, T_ROW:T_ROW + NTILE]
            t.link(V.tensor_reduce(rowc, le2[:, :, 0:E - 1], AX_X, ALU.add))
            t.link(V.tensor_tensor(rowc, io[:, 0:NTILE], rowc, ALU.subtract))
            t.link(V.tensor_scalar(rowc, rowc, float(P), None, ALU.mult))
            t.link(V.scalar_tensor_tensor(rowc, tabf[:, T_WREADY:T_WREADY + NTILE], float(CAP), rowc, ALU.mult, ALU.add))
            t.link(V.tensor_scalar(tabf[:, T_WREADY:T_WREADY + NTILE], tabf[:, T_WREADY:T_WREADY + NTILE], 1.0, None, ALU.add))
            idle = le[:, :, E - 1]
            t.link(V.tensor_scalar(le2[:, :, 0], rowc, -1.0, float(ZROW), ALU.mult, ALU.add))
            t.link(V.tensor_tensor(le2[:, :, 0], le2[:, :, 0], idle, ALU.mult))
            t.link(V.tensor_tensor(rowc, rowc, le2[:, :, 0], ALU.add))
            t.link(V.tensor_tensor(tabf[:, T_PAD:T_PAD + E], n_rows, cape[:, :], ALU.add))
            t.link(V.tensor_scalar(tabf[:, T_FREE:T_FREE + E], upto, 1.0, None, ALU.add))
            for lo, n in ((T_PAR, NTILE), (T_WREADY, NTILE), (T_ROW, NTILE)):
                t.link(V.tensor_copy(tab[:, lo:lo + n], tabf[:, lo:lo + n]))
            V.tensor_copy(tab[:, T_PAD:T_END], tabf[:, T_PAD:T_END]).then_inc(table_ready, 1)
            t.link(V.tensor_tensor(base, upto, n_tiles, ALU.subtract))
            t.close()
            m = Chain(dve, dve_m, 14, 0)
            m.link(V.scalar_tensor_tensor(base, base, float(P), cape[:, :], ALU.mult, ALU.subtract))
            m.link(V.tensor_tensor(ohm, oh_all[:, :, :, :].rearrange("p a t e -> p (a t) e"), experts(base, 2 * NT), ALU.mult))
            m.link(V.tensor_reduce(small[:, 0:2, :].rearrange("p a t -> p (a t)"), ohm, AX_X, ALU.add))
            m.link(V.tensor_tensor(slot_all[:, :, :], slot_all[:, :, :], small[:, 0:2, :].rearrange("p a t -> p t a"), ALU.add))
            m.link(V.tensor_copy(yrow_i[:, :, :], slot_all[:, :, :]))
            V.tensor_tensor(expo, lg_all[:, :, :], m_all[:, :].unsqueeze(2).broadcast_to([P, NT, E]),
                            ALU.subtract).then_inc(exp_in, 1)
            dve.wait_ge(exp_done, 1)
            m.link(V.tensor_reduce(small[:, 2, :], expo2, AX_X, ALU.add))
            m.link(V.reciprocal(small[:, 2, :], small[:, 2, :]))
            m.link(V.tensor_tensor(expo2, expo2, small[:, 2, :].unsqueeze(2).broadcast_to([P, NT, E]), ALU.mult))
            for n in range(2):
                m.link(V.tensor_tensor(expo, expo2, oh_all[:, n, :, :], ALU.mult))
                m.link(V.tensor_reduce(wmix[:, n, :], expo, AX_X, ALU.add))
            m.link(V.tensor_tensor(small[:, 3, :], wmix[:, 0, :], wmix[:, 1, :], ALU.add))
            m.link(V.reciprocal(small[:, 3, :], small[:, 3, :]))
            V.tensor_tensor(wmix[:, :, :], wmix[:, :, :], small[:, 3, :].unsqueeze(1).broadcast_to([P, 2, NT]),
                            ALU.mult).then_inc(mix_ready, 1)

            def low_rows(t):
                dve.wait_ge(rT_high, t + 1)
                V.tensor_tensor(xT[:, 0, 1, :, :], ps_rT[:, :].rearrange("p (k c) -> p k c", c=P),
                                xT[:, 0, 0, :, :].bitcast(F32), ALU.subtract).then_inc(rT_low, 1)

            def gate(t):
                dve.wait_ge(up_done, 2 * t + 2)
                dve.wait_ge(silu_done, t + 1)
                V.tensor_tensor(hid, ps_u[:, :], sg, ALU.mult).then_inc(hid_ready, 1)

            def low_hid(t):
                dve.wait_ge(hT_high, t + 1)
                V.tensor_tensor(hT[:, 1, :, :], ps_hT[:, :].rearrange("p (k c) -> p k c", c=P),
                                hT[:, 0, :, :].bitcast(F32), ALU.subtract).then_inc(hT_low, 1)

            low_rows(0)
            gate(0)
            low_rows(1)
            low_hid(0)
            with dve.Fori(1, NTILE - 1) as i:
                gate(i)
                low_rows(i + 1)
                low_hid(i)
            gate(NTILE - 1)
            low_hid(NTILE - 1)

            def mix(i, s, nth):
                dve.wait_ge(fetched[s], 32 * (nth + 1))
                xi = x1[:, ds(i, 1), :].rearrange("p a d -> p (a d)")
                V.scalar_tensor_tensor(xi, ctxq[:, s, :], wmix[:, 0, ds(i, 1)], xi, ALU.mult, ALU.add).then_inc(mixed, 1)
                dve.wait_ge(mixed, i + 1)
                V.scalar_tensor_tensor(xi, xq[:, s, :], wmix[:, 1, ds(i, 1)], xi, ALU.mult, ALU.add).then_inc(row_ready, 1)

            dve.wait_ge(mix_ready, 1)
            with dve.Fori(0, NT // TB) as q:
                for s in range(TB):
                    mix(TB * q + s, s, q)

        @block.tensor
        def _(pe):
            def attention(b, first=False):
                pe.wait_ge(ctx_ready, NB * (b + 1))
                for k in range(KC):
                    if not (first and k < 2):
                        pe.wait_ge(cT_low, KC * b + k - 1)
                    for j in range(TB):
                        last = nc.tensor.transpose(ps_cT[k % 2][:, j * P:(j + 1) * P], ctxq[:, j, k * P:(k + 1) * P],
                                                   ident[:, :])
                    last.then_inc(cT_formed, 1)

                def turn(j):
                    pe.wait_ge(xq_ready, NB * b + KC * (j + 1))
                    if not (first and j < 2):
                        pe.wait_ge(xT_low, TB * b + j - 1)
                    for k in range(KC):
                        last = nc.tensor.transpose(ps_xT[j % 2][:, k * P:(k + 1) * P], xq[:, j, k * P:(k + 1) * P],
                                                   ident[:, :])
                    last.then_inc(xT_formed, 1)

                turn(0)
                for j in range(TB):
                    if j + 1 < TB:
                        turn(j + 1)
                    if j == 0:
                        pe.wait_ge(cT_low, KC * (b + 1))
                    pe.wait_ge(xT_low, TB * b + j + 1)
                    if not (first and j < 2):
                        pe.wait_ge(x1_ready, TB * b + j - 1)
                    n = 0
                    for k in range(KC):
                        for xp, cp in ((0, 0), (0, 1), (1, 0)):
                            last = nc.tensor.matmul(ps_at[j % 2][:, :], xT[:, j % 2, xp, k, :], cT[:, cp, k, :],
                                                    start=(n == 0), stop=(n == 3 * KC - 1))
                            n += 1
                    last.then_inc(attn_done, 1)

            def router(b, first=False):
                for j in range(TB):
                    pe.wait_ge(y2_ready, TB * b + j + 1)
                    if not (first and j == 0):
                        pe.wait_ge(yT_ready, TB * b + j)
                    for k in range(KC):
                        last = nc.tensor.transpose(ps_yT[:, k * P:(k + 1) * P], y2[:, j, k * P:(k + 1) * P], ident[:, :])
                    last.then_inc(yT_formed, 1)
                    pe.wait_ge(yT_ready, TB * b + j + 1)
                    for k in range(KC):
                        last = nc.tensor.matmul(ps_small[:, j * E:(j + 1) * E], y2T[:, k, :], wr[:, k, :],
                                                start=(k == 0), stop=(k == KC - 1))
                last.then_inc(logits_done, 1)

            def ranks(b):
                pe.wait_ge(chosen, b + 1)
                nc.tensor.matmul(ps_small[:, TB * E:2 * TB * E], before[:, :], selb[:, :, :].rearrange("p t e -> p (t e)"),
                                 start=True, stop=False)
                nc.tensor.matmul(ps_small[:, TB * E:2 * TB * E], ones[:, :], cum[:, 0:TB, :].rearrange("p t e -> p (t e)"),
                                 start=False, stop=True).then_inc(ranks_done, 1)

            pe.wait_ge(masks_ready, 2)
            pe.wait_ge(wr_loaded, 16)
            attention(0, True)
            router(0, True)
            ranks(0)
            with pe.Fori(1, B) as b:
                attention(b)
                pe.wait_ge(slots_ready, b)
                router(b)
                ranks(b)
            pe.wait_ge(slots_ready, B)
            nc.tensor.matmul(ps_small[:, 0:E], ones[:, :], cum[:, TB, :], start=True, stop=True).then_inc(counts_done, 1)

            def turn_rows(t):
                pe.wait_ge(rows_loaded, 16 * (t + 1))
                for k in range(KC):
                    last = nc.tensor.transpose(ps_rT[:, k * P:(k + 1) * P], rows[:, k * P:(k + 1) * P], ident[:, :])
                return last

            def expert_of(t):
                return pe.value_load(tab[0:1, ds(T_PAR + t, 1)], min_val=0, max_val=1)

            def gate_up(t):
                slot_ = expert_of(t)
                ready = pe.value_load(tab[0:1, ds(T_WREADY + t, 1)], min_val=1, max_val=E)
                pe.wait_ge(w_ready, ready)
                pe.wait_ge(rT_low, t + 1)
                for m, bank in ((0, ps_g), (1, ps_u)):
                    n = 0
                    for k in range(KC):
                        for xp, wp in ((0, 0), (0, 1), (1, 0)):
                            last = nc.tensor.matmul(bank[:, :], xT[:, 0, xp, k, :], wsplit[:, ds(slot_, 1), m, wp, k, :],
                                                    start=(n == 0), stop=(n == 3 * KC - 1))
                            n += 1
                    last.then_inc(up_done, 1)

            def down(t, first=False):
                slot_ = expert_of(t)
                pe.wait_ge(hT_low, t + 1)
                if not first:
                    pe.wait_ge(yt_ready, t)
                n = 0
                for k in range(KC):
                    for hp, wp in ((0, 0), (0, 1), (1, 0)):
                        last = nc.tensor.matmul(ps_y[:, :], hT[:, hp, k, :], wsplit[:, ds(slot_, 1), 2, wp, k, :],
                                                start=(n == 0), stop=(n == 3 * KC - 1))
                        n += 1
                last.then_inc(tiles_done, 1)

            def turn_hid(t):
                pe.wait_ge(hid_ready, t + 1)
                for k in range(KC):
                    last = nc.tensor.transpose(ps_hT[:, k * P:(k + 1) * P], hid[:, k * P:(k + 1) * P], ident[:, :])
                last.then_inc(hT_formed, 1)

            pe.wait_ge(table_ready, 1)
            turn_rows(0).then_inc(rT_formed, 1)
            nc.tensor.matmul(ps_small[:, 0:E], ones[:, :], cum[:, TB, :], start=True, stop=True).then_inc(tiles_done, 1)
            gate_up(0)
            turn_rows(1).then_inc(rT_formed, 1)
            turn_hid(0)
            gate_up(1)
            pe.wait_ge(rT_low, 2)
            turn_rows(2).then_inc(rT_formed, 1)
            down(0, True)
            turn_hid(1)
            with pe.Fori(2, NTILE - 1) as t:
                gate_up(t)
                turn_rows(t + 1).then_inc(rT_formed, 1)
                down(t - 1)
                turn_hid(t)
            gate_up(NTILE - 1)
            down(NTILE - 2)
            turn_hid(NTILE - 1)
            down(NTILE - 1)


_INS = ['x', 'ctx_2048', 'L0_ffn_Wr', 'L0_ffn_Wg', 'L0_ffn_Wu', 'L0_ffn_Wd']
_OUTS = [((4, 512, 512), 'float32')]


def kernel(**inputs):
    import numpy as _np
    import concourse.bacc as _bacc
    from concourse import mybir as _mybir
    from concourse.bass_utils import run_bass_kernel_spmd as _run

    nc = _bacc.Bacc("TRN2", target_bir_lowering=False, num_devices=1)
    arrays, args = {}, []
    for name in _INS:
        a = _np.ascontiguousarray(inputs[name])
        arrays[f"in_{name}_dram"] = a
        args.append(nc.dram_tensor(f"in_{name}_dram", a.shape, _mybir.dt.from_np(a.dtype), kind="ExternalInput").ap())
    for i, (shape, dtype) in enumerate(_OUTS):
        dt = _mybir.dt.from_np(_np.dtype(dtype))
        args.append(nc.dram_tensor(f"out_{i}_dram", shape, dt, kind="ExternalOutput").ap())
    xattn_moe(nc, *args)
    r = _run(nc, [arrays], core_ids=[0])
    return r.results[0]["out_0_dram"]
```

```python
from contextlib import ExitStack

import concourse.bass as bass
from concourse import mybir

F32 = mybir.dt.float32
F32R = mybir.dt.float32r
BF16 = mybir.dt.bfloat16
I32 = mybir.dt.int32
U32 = mybir.dt.uint32
ALU = mybir.AluOpType
ACT = mybir.ActivationFunctionType
AX_X = mybir.AxisListType.X
ds = bass.ds

P = 128
B, S, D = 4, 512, 512
E, F, TOPK = 8, 512, 2
KC = D // P
TB = S // P
NT = B * TB
LN_EPS = 1e-5
FP8_MAX, ACT_EPS, W_EPS = 448.0, 1e-4, 1e-6

CAP = B * S + P
ZROW = E * CAP
NTILE = (TOPK * B * S + E * (P - 1)) // P
NFULL = TOPK * B * S // P
FLIGHT = 8
T_PAR, T_WREADY, T_ROW, T_PAD, T_FREE, T_LAST, T_LOW, T_TILES, T_END = 0, 40, 80, 120, 128, 136, 138, 139, 140

EXP_MASK = 0x7F800000
MIN_NORMAL = 2.0 ** -6
ROUND_AT = 1.5 * 2.0 ** 20


class Chain:

    def __init__(self, eng, sem, per, i):
        self.eng, self.sem, self.per, self.start, self.n = eng, sem, per, i * per, 0

    def add(self, ins):
        ins.then_inc(self.sem, 1)
        self.n += 1

    def sync(self):
        self.eng.wait_ge(self.sem, self.start + self.n)

    def sync_alone(self, wait_alone):
        wait_alone(self.eng, self.sem, self.start + self.n)

    def link(self, ins):
        self.add(ins)
        self.sync()

    def close(self):
        assert self.n == self.per, (self.n, self.per)


def xattn_moe(nc, x, ctx_in, Wr, Wg, Wu, Wd, out):
    with ExitStack() as ctx:
        def sb(name, shape, dt):
            return ctx.enter_context(nc.sbuf_tensor(name, shape, dt))

        def sem(name):
            return ctx.enter_context(nc.semaphore(name))

        x1 = sb("x1", [P, NT, D], F32)
        wsplit = sb("wsplit", [P, 2, 3, 2, KC, F], F32R)
        wraw = sb("wraw", [P, 2, KC, F], F32)
        cxq = sb("cxq", [P, 2 * TB, D], F32)
        ctxq = cxq[:, 0:TB, :]
        xq = cxq[:, TB:2 * TB, :]
        magx = sb("magx", [P, 2, D], F32)
        magc = sb("magc", [P, 2, D], F32)
        y2_even = sb("y2_even", [P, TB, D], F32)
        y2T = sb("y2T", [P, 2, KC, P], F32)
        xT = sb("xT", [P, TB, 2, KC, P], F32R)
        wr = sb("wr", [P, KC, E], F32)
        ident = sb("ident", [P, P], F32)
        before = sb("before", [P, P], BF16)
        ones = sb("ones", [P, P], BF16)
        iot = sb("iot", [P, 64], I32)
        alti = sb("alti", [P, E], I32)
        io = sb("io", [P, 64], F32)
        alt = sb("alt", [P, E], F32)
        rev = sb("rev", [P, E], F32)
        cape = sb("cape", [P, E], F32)
        eps = sb("eps", [P, 1], F32)
        stats = sb("stats", [P, 2, TB, 6], F32)
        mv = sb("mv", [P, 2, TB, 2], F32)
        sd = sb("sd", [P, 2, TB], F32)
        rstd = sb("rstd", [P, 2, TB], F32)
        nmr = sb("nmr", [P, 2, TB], F32)
        NB = TB * KC
        xmax = sb("xmax", [P, NB], F32)
        xsc = sb("xsc", [P, NB], F32)
        xinv = sb("xinv", [P, NB], F32)
        cmaxp = sb("cmaxp", [P, NB], F32)
        cmax = sb("cmax", [P, NB], F32)
        csc = sb("csc", [P, NB], F32)
        cinv = sb("cinv", [P, NB], F32)
        rl = sb("rl", [P, TB, E], F32)
        rl2 = sb("rl2", [P, TB, E], F32)
        eq = sb("eq", [P, TB, E], F32)
        top = sb("top", [P, 2, TB], F32)
        pick = sb("pick", [P, 2, TB], F32)
        oh = sb("oh", [P, 2, TB, E], F32)
        selb = sb("selb", [P, TB, E], BF16)
        cum = sb("cum", [P, TB + 1, E], BF16)
        place = sb("place", [P, TB, E], F32)
        slot = sb("slot", [P, TB, 2], F32)
        slot_i = sb("slot_i", [P, TB, 2], I32)
        oh_all = sb("oh_all", [P, 2, NT, E], F32)
        slot_all = sb("slot_all", [P, NT, 2], F32)
        lg_all = sb("lg_all", [P, NT, E], F32)
        m_all = sb("m_all", [P, NT], F32)
        yrow_i = sb("yrow_i", [P, NT, 2], I32)
        wmix = sb("wmix", [P, 2, NT], F32)
        count = sb("count", [P, 4, E], F32)
        tabf = sb("tabf", [P, T_END], F32)
        tab = sb("tab", [P, T_END], I32)
        small = sb("small", [P, 6, NT], F32)

        cT = wsplit[:, 1, 0, :, :, :]
        y2 = (y2_even, wraw[:, 1, :, :])
        rows, hid = magx[:, 0, :], magx[:, 1, :]
        sg, yt = magc[:, 0, :], magc[:, 1, :]
        rT, hT = xT[:, 0, :, :, :], xT[:, 1, :, :, :]
        zero = xq[:, 0, :]
        blank = wsplit[:, 0, 2, 1, 0, :].bitcast(F32)
        fetch_buf = (wraw[:, :, :, :].rearrange("p s k f -> p (s k) f"), cxq)
        spare = ctxq[:, :, :].rearrange("p t d -> p (t d)")
        le = spare[:, 0:NTILE * E].rearrange("p (t e) -> p t e", e=E)
        le2 = spare[:, 512:512 + NTILE * E].rearrange("p (t e) -> p t e", e=E)
        over = spare[:, 1024:1024 + E * NT].rearrange("p (e j) -> p e j", j=NT)
        expo = spare[:, 1152:1152 + NT * E].rearrange("p (t e) -> p t e", e=E)
        expo2 = spare[:, 1280:1280 + NT * E].rearrange("p (t e) -> p t e", e=E)
        ohm = spare[:, 1408:1408 + 2 * NT * E].rearrange("p (a e) -> p a e", e=E)

        ps = [ctx.enter_context(nc.psum_tensor(f"ps{i}", [P, 512], F32)) for i in range(8)]
        ps_T, ps_at, ps_yT, ps_small = ps[0:4], ps[4:6], (ps[6], ps[3]), ps[7]
        ps_g, ps_u, ps_y, ps_hT, ps_rT = ps[0], ps[1], ps[4], ps[5], ps[2]

        grouped = nc.dram_tensor("grouped", [ZROW + P, D], F32, kind="Internal").ap()
        results = nc.dram_tensor("results", [NTILE * P, D], F32, kind="Internal").ap()

        x_rows = x.rearrange("b s d -> (b s) d")
        out_rows = out.rearrange("b s d -> (b s) d")
        weights = (Wg, Wu, Wd)

        x_loaded, ctx_loaded, wr_loaded = sem("x_loaded"), sem("ctx_loaded"), sem("wr_loaded")
        masks_ready, consts_ready, pool_set = sem("masks_ready"), sem("consts_ready"), sem("pool_set")
        dve_const = sem("dve_const")
        ctx_maxed, ctx_max_all, ctx_scaled = sem("ctx_maxed"), sem("ctx_max_all"), sem("ctx_scaled")
        x_scaled, ctx_quant, x_quant = sem("x_scaled"), sem("ctx_quant"), sem("x_quant")
        ln1_var, ln1_sd, ln1_ready, ln1_done = sem("ln1_var"), sem("ln1_sd"), sem("ln1_ready"), sem("ln1_done")
        ctx_biased, ctx_rounded, ctx_ready = sem("ctx_biased"), sem("ctx_rounded"), sem("ctx_ready")
        x_biased, x_rounded, xq_ready = sem("x_biased"), sem("x_rounded"), sem("xq_ready")
        cT_formed, cT_high, cT_low = sem("cT_formed"), sem("cT_high"), sem("cT_low")
        xT_formed, xT_high, xT_low = sem("xT_formed"), sem("xT_high"), sem("xT_low")
        attn_done, x1_ready = sem("attn_done"), sem("x1_ready")
        ln2_var, ln2_sd, ln2_ready, y2_ready = sem("ln2_var"), sem("ln2_sd"), sem("ln2_ready"), sem("y2_ready")
        yT_formed, yT_ready, logits_done = sem("yT_formed"), sem("yT_ready"), sem("logits_done")
        chosen, ranks_done, slots_ready = sem("chosen"), sem("ranks_done"), sem("slots_ready")
        scattered = sem("scattered")
        w_loaded = [sem("w_loaded0"), sem("w_loaded1")]
        w_split, w_ready = sem("w_split"), sem("w_ready")
        counts_done, pads_ready = sem("counts_done"), sem("pads_ready")
        table_ready, zero_ready = sem("table_ready"), sem("zero_ready")
        padded, rows_loaded = sem("padded"), sem("rows_loaded")
        rT_formed, rT_high, rT_low = sem("rT_formed"), sem("rT_high"), sem("rT_low")
        up_done, silu_done, hid_ready = sem("up_done"), sem("silu_done"), sem("hid_ready")
        hT_formed, hT_high, hT_low = sem("hT_formed"), sem("hT_high"), sem("hT_low")
        tiles_done, yt_ready, yt_stored = sem("tiles_done"), sem("yt_ready"), sem("yt_stored")
        exp_in, exp_done, mix_ready = sem("exp_in"), sem("exp_done"), sem("mix_ready")
        fetched_low = sem("fetched_low")
        fetched_high = [sem(f"fetched_high{s}") for s in range(FLIGHT)]
        low_mixed, row_ready, out_stored = sem("low_mixed"), sem("row_ready"), sem("out_stored")
        blank_ready, results_cleared = sem("blank_ready"), sem("results_cleared")
        waited = sem("waited")
        dve_l, dve_q, dve_a = sem("dve_l"), sem("dve_q"), sem("dve_a")
        dve_r, dve_t, dve_m = sem("dve_r"), sem("dve_t"), sem("dve_m")

        def wait_alone(eng, sem_, value):
            eng.wait_ge(sem_, value)
            eng.sem_inc(waited, 1)

        def table_value(eng, column, low, high=NTILE):
            return eng.value_load(tab[0:1, column:column + 1], min_val=low, max_val=high)

        block = ctx.enter_context(nc.Block())

        @block.sync
        def _(sp):
            def load_x(b):
                sp.dma_start(x1[:, TB * b:TB * b + TB, :],
                             x_rows[S * b:S * b + S, :].rearrange("(t p) d -> p t d", p=P)).then_inc(x_loaded, 16)

            def load_ctx(b):
                sp.dma_start(ctxq[:, :, :], ctx_in[b].rearrange("(t p) d -> p t d", p=P)).then_inc(ctx_loaded, 16)

            load_ctx(0)
            load_x(0)
            sp.dma_start(wr[:, :, :], Wr.rearrange("(k p) e -> p k e", p=P)).then_inc(wr_loaded, 16)
            for b in range(1, B):
                sp.wait_ge(x_loaded, 16 * b)
                load_x(b)
            for b in range(1, B):
                sp.wait_ge(cT_formed, TB * b)
                load_ctx(b)
                sp.wait_ge(blank_ready, 1)
                part = NTILE // (B - 1)
                sp.dma_start(results[(b - 1) * part * P:b * part * P, :].rearrange("(t p) d -> p t d", p=P),
                             blank.unsqueeze(1).broadcast_to([P, part, D])).then_inc(results_cleared, 16)

            sp.wait_ge(zero_ready, 1)
            sp.dma_start(grouped[ZROW:ZROW + P, :], zero).then_inc(padded, 16)
            sp.wait_ge(pads_ready, 1)
            for e in range(E):
                pad = sp.value_load(tab[0:1, T_PAD + e:T_PAD + e + 1], min_val=0, max_val=ZROW - P)
                sp.dma_start(grouped[ds(pad, P), :], zero).then_inc(padded, 16)
            sp.wait_ge(padded, 16 * (E + 1))
            sp.wait_ge(table_ready, 1)
            sp.wait_ge(scattered, 16 * 2 * NT)

            def load_rows(t):
                row = sp.value_load(tab[0:1, ds(T_ROW + t, 1)], min_val=0, max_val=ZROW)
                sp.dma_start(rows, grouped[ds(row, P), :]).then_inc(rows_loaded, 16)

            def store_result(t):
                sp.wait_ge(yt_ready, t + 1)
                sp.dma_start(results[ds(t * P, P), :], yt).then_inc(yt_stored, 16)

            load_rows(0)
            sp.wait_ge(rT_formed, 1)
            load_rows(1)
            sp.wait_ge(rT_formed, 2)
            load_rows(2)
            sp.wait_ge(results_cleared, 16 * (B - 1))

            def rows_and_result(t):
                sp.wait_ge(rT_formed, t + 2)
                load_rows(t + 2)
                store_result(t - 1)

            tiles_ = table_value(sp, T_TILES, NFULL)
            with sp.Fori(1, NFULL - 1) as t:
                rows_and_result(t)
            with sp.Fori(NFULL - 1, NTILE - 1) as t:
                with sp.If(t + 1 < tiles_):
                    rows_and_result(t)
            store_result(table_value(sp, T_LAST, NFULL - 2, NTILE - 2))
            store_result(table_value(sp, T_LAST + 1, NFULL - 1, NTILE - 1))

            with sp.Fori(0, NT) as i:
                sp.wait_ge(row_ready, i + 1)
                sp.dma_start(out_rows[ds(i * P, P), :],
                             x1[:, ds(i, 1), :].rearrange("p a d -> p (a d)")).then_inc(out_stored, 16)
            sp.wait_ge(out_stored, 16 * NT)

        @block.gpsimd
        def _(pool):
            nc.gpsimd.memset(ident[:, :], 0.0).then_inc(pool_set, 1)
            nc.gpsimd.memset(before[:, :], 1.0).then_inc(pool_set, 1)
            nc.gpsimd.memset(ones[:, :], 1.0).then_inc(pool_set, 1)
            nc.gpsimd.iota(iot[:, :], pattern=[[1, 64]], base=0, channel_multiplier=0).then_inc(pool_set, 1)
            nc.gpsimd.iota(alti[:, :], pattern=[[0, E // 2], [-2, 2]], base=1, channel_multiplier=0).then_inc(pool_set, 1)
            pool.wait_ge(pool_set, 5)
            nc.gpsimd.affine_select(out=ident[:, :], in_=ident[:, :], compare_op=ALU.not_equal, fill=1.0,
                                    base=0, pattern=[[-1, P]], channel_multiplier=1).then_inc(masks_ready, 1)
            nc.gpsimd.affine_select(out=before[:, :], in_=before[:, :], compare_op=ALU.is_gt, fill=0.0,
                                    base=0, pattern=[[1, P]], channel_multiplier=-1).then_inc(masks_ready, 1)

            def load_weights(e, m, stage):
                src = weights[m][ds(e, 1)].rearrange("a (k p) f -> p (a k) f", p=P)
                pool.dma_start(wraw[:, stage, :, :], src).then_inc(w_loaded[stage], 16)

            def split_weights(m, slot_, stage, nth, count_before, last):
                wait_alone(pool, w_loaded[stage], 16 * (nth + 1))
                high, low = wsplit[:, slot_, m, 0, :, :], wsplit[:, slot_, m, 1, :, :]
                nc.gpsimd.tensor_scalar(high, wraw[:, stage, :, :], 1.0, 1.0, ALU.mult, ALU.mult).then_inc(w_split, 1)
                pool.wait_ge(w_split, count_before + 1)
                nc.gpsimd.tensor_tensor(low, wraw[:, stage, :, :], high.bitcast(F32),
                                        ALU.subtract).then_inc(w_split if last is None else w_ready, 1)
                if last is None:
                    wait_alone(pool, w_split, count_before + 2)
                else:
                    wait_alone(pool, w_ready, last)

            def ctx_max(b):
                pool.wait_ge(ctx_maxed, b + 1)
                nc.gpsimd.partition_all_reduce(cmax[:, :], cmaxp[:, :], P,
                                               bass.bass_isa.ReduceOp.max).then_inc(ctx_max_all, 1)

            def quantise_x(b, j):
                pool.wait_ge(x_scaled, b + 1)
                for k in range(KC):
                    v = xq[:, j, k * P:(k + 1) * P]
                    last = nc.gpsimd.tensor_scalar(v, v, xinv[:, KC * j + k:KC * j + k + 1], 1.0, ALU.mult, ALU.mult)
                last.then_inc(x_quant, 1)

            def round_off(b, j, buf, mag, biased, rounded):
                pool.wait_ge(biased, TB * b + j + 1)
                nc.gpsimd.tensor_tensor(buf[:, j, :], buf[:, j, :], mag[:, j % 2, :], ALU.subtract).then_inc(rounded, 1)

            def quantisation(b):
                ctx_max(b)
                for j in range(TB):
                    round_off(b, j, ctxq, magc, ctx_biased, ctx_rounded)
                    quantise_x(b, j)
                for j in range(TB):
                    round_off(b, j, xq, magx, x_biased, x_rounded)

            def scatter(b):
                pool.wait_ge(slots_ready, b + 1)
                for j in range(TB):
                    for c in range(2):
                        nc.gpsimd.indirect_dma_start(
                            grouped[:, :], bass.IndirectOffsetOnAxis(ap=slot_i[:, j, c:c + 1], axis=0),
                            y2[b % 2][:, j, :], None).then_inc(scattered, 16)

            load_weights(0, 0, 0)
            split_weights(0, 0, 0, 0, 0, None)
            load_weights(0, 1, 0)
            quantisation(0)
            quantisation(1)
            split_weights(1, 0, 0, 1, 2, None)
            load_weights(0, 2, 0)
            quantisation(2)
            scatter(0)
            quantisation(3)
            scatter(1)
            pool.wait_ge(results_cleared, 16 * (B - 1))
            split_weights(2, 0, 0, 2, 4, 1)
            load_weights(1, 0, 0)
            scatter(2)
            scatter(3)
            pool.wait_ge(attn_done, NT)
            split_weights(0, 1, 0, 3, 5, None)
            load_weights(1, 2, 0)
            pool.wait_ge(scattered, 32 * NT)
            load_weights(1, 1, 1)
            split_weights(1, 1, 1, 0, 7, None)
            load_weights(2, 0, 1)
            split_weights(2, 1, 0, 4, 9, 2)
            load_weights(2, 1, 0)
            pool.wait_ge(table_ready, 1)

            def expert(e, slot_, nth0, nth1, before_, first_stage, load_next):
                free = pool.value_load(tab[0:1, ds(T_FREE + e - 2, 1)], min_val=1, max_val=NTILE + 1)
                wait_alone(pool, tiles_done, free)
                a, z = first_stage, 1 - first_stage
                n = [nth0, nth1]
                split_weights(0, slot_, a, n[a], before_, None)
                load_weights(e, 2, a)
                split_weights(1, slot_, z, n[z], before_ + 2, None)
                if load_next:
                    load_weights(e + 1, 0, z)
                split_weights(2, slot_, a, n[a] + 1, before_ + 4, e + 1)
                if load_next:
                    load_weights(e + 1, 1, a)

            with pool.Fori(0, E // 2 - 2) as q:
                expert(2 + 2 * q, 0, 5 + 3 * q, 1 + 3 * q, 10 + 10 * q, 1, True)
                expert(3 + 2 * q, 1, 6 + 3 * q, 3 + 3 * q, 15 + 10 * q, 0, True)
            expert(E - 2, 0, 11, 7, 30, 1, True)
            expert(E - 1, 1, 12, 9, 35, 0, False)

            def fetch(i, which, fetched):
                nc.gpsimd.indirect_dma_start(
                    fetch_buf[i // FLIGHT][:, i % FLIGHT, :], None, results[:, :],
                    bass.IndirectOffsetOnAxis(ap=yrow_i[:, i, which:which + 1], axis=0)).then_inc(fetched, 16)

            pool.wait_ge(mix_ready, 1)
            wait_alone(pool, yt_stored, table_value(pool, T_LOW, NFULL // 2) * 16)
            for i in range(NT):
                fetch(i, 0, fetched_low)
            wait_alone(pool, yt_stored, table_value(pool, T_TILES, NFULL) * 16)
            for i in range(NT):
                pool.wait_ge(low_mixed, i + 1)
                if i >= FLIGHT:
                    pool.wait_ge(row_ready, i - FLIGHT + 1)
                fetch(i, 1, fetched_high[i % FLIGHT])

        @block.scalar
        def _(act):
            def ln1_deviation(b):
                act.wait_ge(ln1_var, b + 1)
                nc.scalar.activation(sd[:, 0, :], mv[:, 0, :, 1], ACT.Sqrt, bias=eps[:, :]).then_inc(ln1_sd, 1)

            def normalise(b, which, ready, out_, done):
                act.wait_ge(ready, b + 1)
                for j in range(TB):
                    nc.scalar.activation(out_[:, j, :], x1[:, TB * b + j, :], ACT.Identity, bias=nmr[:, which, j:j + 1],
                                         scale=rstd[:, which, j:j + 1]).then_inc(done, 1)

            def ln1(b):
                if b > 0:
                    act.wait_ge(xT_formed, TB * b)
                normalise(b, 0, ln1_ready, xq, ln1_done)

            def ln2(b):
                if b >= 2:
                    act.wait_ge(scattered, 32 * TB * (b - 1))
                normalise(b, 1, ln2_ready, y2[b % 2], y2_ready)

            def ln2_deviation(b):
                act.wait_ge(ln2_var, b + 1)
                nc.scalar.activation(sd[:, 1, :], mv[:, 1, :, 1], ACT.Sqrt, bias=eps[:, :]).then_inc(ln2_sd, 1)

            def scale_blocks(b, j, buf, factors, before_, count_before_, after_):
                act.wait_ge(before_, count_before_)
                for k in range(KC):
                    v = buf[:, j, k * P:(k + 1) * P]
                    last = nc.scalar.activation(v, v, ACT.Copy, scale=factors[:, KC * j + k:KC * j + k + 1])
                last.then_inc(after_, 1)

            def quantise_ctx(b, j):
                scale_blocks(b, j, ctxq, cinv, ctx_scaled, b + 1, ctx_quant)

            def dequantise(b):
                for j in range(TB):
                    scale_blocks(b, j, ctxq, csc, ctx_rounded, TB * b + j + 1, ctx_ready)
                for j in range(TB):
                    scale_blocks(b, j, xq, xsc, x_rounded, TB * b + j + 1, xq_ready)

            def high_parts(b):
                for k in range(KC):
                    act.wait_ge(cT_formed, KC * b + k + 1)
                    nc.scalar.activation(cT[:, 0, k, :], ps_T[k][:, :], ACT.Copy).then_inc(cT_high, 1)
                for j in range(TB):
                    act.wait_ge(xT_formed, TB * b + j + 1)
                    nc.scalar.activation(xT[:, j, 0, :, :], ps_T[j][:, :].rearrange("p (k c) -> p k c", c=P),
                                         ACT.Copy).then_inc(xT_high, 1)

            def transposed_y2(b, j):
                act.wait_ge(yT_formed, TB * b + j + 1)
                nc.scalar.activation(y2T[:, j % 2, :, :], ps_yT[j % 2][:, :].rearrange("p (k c) -> p k c", c=P),
                                     ACT.Copy).then_inc(yT_ready, 1)

            act.wait_ge(consts_ready, 1)
            ln1_deviation(0)
            ln1(0)
            for j in range(TB):
                quantise_ctx(0, j)
            ln1_deviation(1)
            dequantise(0)
            for b in range(B):
                high_parts(b)
                if b + 1 < B:
                    ln1(b + 1)
                if b >= 1:
                    ln2(b - 1)
                for j in range(TB):
                    if b >= 1:
                        transposed_y2(b - 1, j)
                    if b + 1 < B:
                        quantise_ctx(b + 1, j)
                if b + 2 < B:
                    ln1_deviation(b + 2)
                if b + 1 < B:
                    dequantise(b + 1)
                ln2_deviation(b)
            ln2(B - 1)
            for j in range(TB):
                transposed_y2(B - 1, j)

            act.wait_ge(exp_in, 1)
            nc.scalar.activation(expo2, expo, ACT.Exp).then_inc(exp_done, 1)

            def high_rows(t):
                act.wait_ge(rT_formed, t + 1)
                nc.scalar.activation(rT[:, 0, :, :], ps_rT[:, :].rearrange("p (k c) -> p k c", c=P),
                                     ACT.Copy).then_inc(rT_high, 1)

            def silu(t):
                act.wait_ge(up_done, 2 * t + 1)
                nc.scalar.activation(sg, ps_g[:, :], ACT.Silu).then_inc(silu_done, 1)

            def high_hid(t):
                act.wait_ge(hT_formed, t + 1)
                nc.scalar.activation(hT[:, 0, :, :], ps_hT[:, :].rearrange("p (k c) -> p k c", c=P),
                                     ACT.Copy).then_inc(hT_high, 1)

            def result(t, first=False):
                act.wait_ge(tiles_done, t + 2)
                if not first:
                    act.wait_ge(yt_stored, 16 * t)
                nc.scalar.activation(yt, ps_y[:, :], ACT.Copy).then_inc(yt_ready, 1)

            high_rows(0)
            silu(0)
            high_rows(1)
            high_hid(0)
            silu(1)
            high_rows(2)
            result(0, True)
            high_hid(1)

            def tile(t):
                act.wait_ge(hid_ready, t)
                silu(t)
                high_rows(t + 1)
                result(t - 1)
                high_hid(t)

            tiles_ = table_value(act, T_TILES, NFULL)
            with act.Fori(2, NFULL) as t:
                tile(t)
            with act.Fori(NFULL, NTILE) as t:
                with act.If(t < tiles_):
                    tile(t)
            result(table_value(act, T_LAST + 1, NFULL - 1, NTILE - 1))

        @block.vector
        def _(dve):
            V = nc.vector
            dve.wait_ge(masks_ready, 2)
            c = Chain(dve, dve_const, 7, 0)
            c.add(V.tensor_copy(io[:, :], iot[:, :]))
            c.add(V.tensor_copy(alt[:, :], alti[:, :]))
            c.add(V.memset(eps[:, :], LN_EPS))
            c.add(V.memset(cum[:, TB, :], 0.0))
            c.sync()
            c.add(V.tensor_scalar(rev[:, :], io[:, 0:E], -1.0, float(E), ALU.mult, ALU.add))
            c.add(V.tensor_scalar(cape[:, :], io[:, 0:E], float(CAP), None, ALU.mult))
            c.add(V.memset(small[:, 0, :], 0.0))
            c.close()
            c.sync()
            V.memset(small[:, 1, :], 0.0).then_inc(consts_ready, 1)
            V.memset(blank, 0.0).then_inc(blank_ready, 1)

            def tiles(ap):
                return ap.unsqueeze(2).broadcast_to([P, TB, E])

            def experts(ap, n=TB):
                return ap.unsqueeze(1).broadcast_to([P, n, E])

            def block_max(out_, buf):
                return V.tensor_reduce(out_[:, :], buf[:, :, :].rearrange("p t (k c) -> p (t k) c", c=P), AX_X, ALU.max,
                                       apply_absolute_value=True)

            def ln_stats(c, which, b, j):
                c.add(V.bn_stats(stats[:, which, j, :], x1[:, TB * b + j, :]))

            def ln_aggregate(c, which, var_ready):
                c.sync()
                for j in range(TB):
                    last = V.bn_aggr(mv[:, which, j, :], stats[:, which, j, :])
                    if j < TB - 1:
                        c.add(last)
                last.then_inc(var_ready, 1)

            def ln_scale(c, which, sd_sem, b, ready):
                dve.wait_ge(sd_sem, b + 1)
                c.link(V.reciprocal(rstd[:, which, :], sd[:, which, :]))
                V.scalar_tensor_tensor(nmr[:, which, :], mv[:, which, :, 0], -1.0, rstd[:, which, :],
                                       ALU.mult, ALU.mult).then_inc(ready, 1)

            def scales(c, maxima, scale, inv, floor, ready):
                c.link(V.tensor_scalar(maxima[:, :], maxima[:, :], floor, None, ALU.max))
                c.add(V.tensor_scalar(scale[:, :], maxima[:, :], 1.0 / FP8_MAX, None, ALU.mult))
                c.link(V.reciprocal(inv[:, :], maxima[:, :]))
                V.tensor_scalar(inv[:, :], inv[:, :], FP8_MAX, None, ALU.mult).then_inc(ready, 1)

            def ln1_stats(c, b):
                dve.wait_ge(x_loaded, 16 * (b + 1))
                for j in range(TB):
                    ln_stats(c, 0, b, j)
                ln_aggregate(c, 0, ln1_var)

            def maxima(c, b):
                dve.wait_ge(ctx_loaded, 16 * (b + 1))
                block_max(cmaxp, ctxq).then_inc(ctx_maxed, 1)
                dve.wait_ge(ln1_done, TB * (b + 1))
                c.link(block_max(xmax, xq))
                dve.wait_ge(ctx_max_all, b + 1)
                scales(c, cmax, csc, cinv, W_EPS, ctx_scaled)
                scales(c, xmax, xsc, xinv, ACT_EPS, x_scaled)

            def to_grid(c, b, j, buf, mag, quantised, rounded, biased):
                v, m = buf[:, j, :], mag[:, j % 2, :]
                dve.wait_ge(quantised, TB * b + j + 1)
                if TB * b + j >= 2:
                    dve.wait_ge(rounded, TB * b + j - 1)
                c.link(V.tensor_scalar(m.bitcast(U32), v.bitcast(U32), EXP_MASK, None, ALU.bitwise_and))
                c.link(V.tensor_scalar(m, m, MIN_NORMAL, ROUND_AT, ALU.max, ALU.mult))
                V.tensor_tensor(v, v, m, ALU.add).then_inc(biased, 1)

            def ctx_to_grid(c, b, j):
                to_grid(c, b, j, ctxq, magc, ctx_quant, ctx_rounded, ctx_biased)

            def x_to_grid(c, b, j):
                to_grid(c, b, j, xq, magx, x_quant, x_rounded, x_biased)

            NL1, NL2, NQ = 4 + 3 + 1, 4 + 3 + 1, 1 + 3 + 3 + 2 * 2 * TB

            def low_ctx(b):
                for k in range(KC):
                    dve.wait_ge(cT_high, KC * b + k + 1)
                    V.tensor_tensor(cT[:, 1, k, :], ps_T[k][:, :], cT[:, 0, k, :].bitcast(F32),
                                    ALU.subtract).then_inc(cT_low, 1)

            def low_x(b):
                for j in range(TB):
                    dve.wait_ge(xT_high, TB * b + j + 1)
                    V.tensor_tensor(xT[:, j, 1, :, :], ps_T[j][:, :].rearrange("p (k c) -> p k c", c=P),
                                    xT[:, j, 0, :, :].bitcast(F32), ALU.subtract).then_inc(xT_low, 1)

            def add_attention(a, b, j):
                dve.wait_ge(attn_done, TB * b + j + 1)
                V.tensor_tensor(x1[:, TB * b + j, :], ps_at[j % 2][:, :], x1[:, TB * b + j, :],
                                ALU.add).then_inc(x1_ready, 1)
                dve.wait_ge(x1_ready, TB * b + j + 1)
                ln_stats(a, 1, b, j)

            NR = 27

            def choose(r, b):
                dve.wait_ge(logits_done, b + 1)
                r.add(V.tensor_copy(rl[:, :, :], ps_small[:, 0:TB * E].rearrange("p (t e) -> p t e", e=E)))
                r.add(V.tensor_copy(cum[:, 0, :], cum[:, TB, :]))
                r.sync()
                src = rl
                for n in range(2):
                    r.link(V.tensor_reduce(top[:, n, :], src[:, :, :], AX_X, ALU.max))
                    r.link(V.tensor_tensor(eq[:, :, :], src[:, :, :], tiles(top[:, n, :]), ALU.is_equal))
                    r.link(V.tensor_tensor(eq[:, :, :], eq[:, :, :], experts(rev[:, :]), ALU.mult))
                    r.link(V.tensor_reduce(pick[:, n, :], eq[:, :, :], AX_X, ALU.max))
                    r.link(V.tensor_tensor(oh[:, n, :, :], experts(rev[:, :]), tiles(pick[:, n, :]), ALU.is_equal))
                    if n == 0:
                        r.link(V.scalar_tensor_tensor(rl2[:, :, :], oh[:, 0, :, :], -3.0e38, rl[:, :, :], ALU.mult, ALU.add))
                        src = rl2
                r.link(V.tensor_tensor(selb[:, :, :], oh[:, 0, :, :], oh[:, 1, :, :], ALU.add))
                for j in range(TB):
                    last = V.tensor_tensor(cum[:, j + 1, :], cum[:, j, :], selb[:, j, :], ALU.add)
                    if j < TB - 1:
                        r.link(last)
                last.then_inc(chosen, 1)

            def give_slots(r, b):
                for n in range(2):
                    r.add(V.tensor_copy(oh_all[:, n, TB * b:TB * b + TB, :], oh[:, n, :, :]))
                r.add(V.tensor_copy(lg_all[:, TB * b:TB * b + TB, :], rl[:, :, :]))
                r.add(V.tensor_copy(m_all[:, TB * b:TB * b + TB], top[:, 0, :]))
                dve.wait_ge(ranks_done, b + 1)
                r.link(V.tensor_tensor(place[:, :, :], ps_small[:, TB * E:2 * TB * E].rearrange("p (t e) -> p t e", e=E),
                                       experts(cape[:, :]), ALU.add))
                for n in range(2):
                    r.link(V.tensor_tensor(eq[:, :, :], oh[:, n, :, :], place[:, :, :], ALU.mult))
                    r.link(V.tensor_reduce(slot[:, :, n], eq[:, :, :], AX_X, ALU.add))
                r.add(V.tensor_copy(slot_all[:, TB * b:TB * b + TB, :], slot[:, :, :]))

                if b > 0:
                    dve.wait_ge(scattered, 32 * TB * b)
                V.tensor_copy(slot_i[:, :, :], slot[:, :, :]).then_inc(slots_ready, 1)
                r.close()

            def first_layernorm(b):
                c = Chain(dve, dve_l, NL1, b)
                ln1_stats(c, b)
                return c

            first = first_layernorm(0)
            ln_scale(first, 0, ln1_sd, 0, ln1_ready)
            c = Chain(dve, dve_q, NQ, 0)
            maxima(c, 0)
            first = first_layernorm(1)
            for j in range(TB):
                ctx_to_grid(c, 0, j)
            ln_scale(first, 0, ln1_sd, 1, ln1_ready)
            for j in range(TB):
                x_to_grid(c, 0, j)
            c.close()
            second = None
            for b in range(B):
                low_ctx(b)
                if b >= 1:
                    ln_scale(second, 1, ln2_sd, b - 1, ln2_ready)
                    second.close()
                    r = Chain(dve, dve_r, NR, b - 1)
                low_x(b)
                if b + 2 < B:
                    first = first_layernorm(b + 2)
                second = Chain(dve, dve_a, NL2, b)
                if b + 1 < B:
                    c = Chain(dve, dve_q, NQ, b + 1)
                    maxima(c, b + 1)
                    ctx_to_grid(c, b + 1, 0)
                    ctx_to_grid(c, b + 1, 1)
                if b + 2 < B:
                    ln_scale(first, 0, ln1_sd, b + 2, ln1_ready)
                    first.close()
                if b >= 1 and b + 1 < B:
                    choose(r, b - 1)
                if b + 1 < B:
                    ctx_to_grid(c, b + 1, 2)
                    ctx_to_grid(c, b + 1, 3)
                for j in range(TB):
                    add_attention(second, b, j)
                    if b + 1 < B:
                        x_to_grid(c, b + 1, j)
                    if b >= 1 and b + 1 < B and j == 1:
                        give_slots(r, b - 1)
                ln_aggregate(second, 1, ln2_var)
                if b + 1 < B:
                    c.close()
            ln_scale(second, 1, ln2_sd, B - 1, ln2_ready)
            second.close()
            choose(r, B - 2)
            give_slots(r, B - 2)
            V.memset(zero, 0.0).then_inc(zero_ready, 1)
            r = Chain(dve, dve_r, NR, B - 1)
            choose(r, B - 1)
            give_slots(r, B - 1)

            n_rows, n_tiles, upto, base = (count[:, i, :] for i in range(4))
            t = Chain(dve, dve_t, 33, 0)
            dve.wait_ge(counts_done, 1)
            t.link(V.tensor_copy(n_rows, ps_small[:, 0:E]))
            t.link(V.tensor_tensor(tabf[:, T_PAD:T_PAD + E], n_rows, cape[:, :], ALU.add))
            V.tensor_copy(tab[:, T_PAD:T_PAD + E], tabf[:, T_PAD:T_PAD + E]).then_inc(pads_ready, 1)
            t.link(V.tensor_scalar(tabf[:, 0:NT], io[:, 0:NT], float(P), None, ALU.mult))
            t.link(V.tensor_tensor(over, n_rows.unsqueeze(2).broadcast_to([P, E, NT]),
                                   tabf[:, 0:NT].unsqueeze(1).broadcast_to([P, E, NT]), ALU.is_gt))
            t.link(V.tensor_reduce(n_tiles, over, AX_X, ALU.add))
            t.link(V.tensor_copy(upto[:, 0:1], n_tiles[:, 0:1]))
            for e in range(1, E):
                t.link(V.tensor_tensor(upto[:, e:e + 1], upto[:, e - 1:e], n_tiles[:, e:e + 1], ALU.add))
            tcol = io[:, 0:NTILE].unsqueeze(2).broadcast_to([P, NTILE, E])
            t.link(V.tensor_tensor(le, tcol, experts(upto, NTILE), ALU.is_ge))
            t.link(V.tensor_tensor(le2, le, experts(alt[:, :], NTILE), ALU.mult))
            t.link(V.tensor_reduce(tabf[:, T_PAR:T_PAR + NTILE], le2[:, :, 0:E - 1], AX_X, ALU.add))
            t.link(V.tensor_reduce(tabf[:, T_WREADY:T_WREADY + NTILE], le[:, :, 0:E - 1], AX_X, ALU.add))
            t.link(V.tensor_tensor(le2, le, experts(n_tiles, NTILE), ALU.mult))
            rowc = tabf[:, T_ROW:T_ROW + NTILE]
            t.link(V.tensor_reduce(rowc, le2[:, :, 0:E - 1], AX_X, ALU.add))
            t.link(V.tensor_tensor(rowc, io[:, 0:NTILE], rowc, ALU.subtract))
            t.link(V.tensor_scalar(rowc, rowc, float(P), None, ALU.mult))
            t.link(V.scalar_tensor_tensor(rowc, tabf[:, T_WREADY:T_WREADY + NTILE], float(CAP), rowc, ALU.mult, ALU.add))
            t.link(V.tensor_scalar(tabf[:, T_WREADY:T_WREADY + NTILE], tabf[:, T_WREADY:T_WREADY + NTILE], 1.0, None, ALU.add))
            idle = le[:, :, E - 1]
            t.link(V.tensor_scalar(le2[:, :, 0], rowc, -1.0, float(ZROW), ALU.mult, ALU.add))
            t.link(V.tensor_tensor(le2[:, :, 0], le2[:, :, 0], idle, ALU.mult))
            t.link(V.tensor_tensor(rowc, rowc, le2[:, :, 0], ALU.add))
            t.link(V.tensor_scalar(tabf[:, T_FREE:T_FREE + E], upto, 1.0, None, ALU.add))
            t.link(V.tensor_tensor(tabf[:, T_LAST:T_LAST + 2], upto[:, E - 1:E].broadcast_to([P, 2]), rev[:, E - 2:E],
                                   ALU.subtract))
            t.link(V.tensor_copy(tabf[:, T_LOW:T_TILES + 1], upto[:, E - 2:E]))
            for lo, n in ((T_PAR, NTILE), (T_WREADY, NTILE), (T_ROW, NTILE)):
                t.link(V.tensor_copy(tab[:, lo:lo + n], tabf[:, lo:lo + n]))
            V.tensor_copy(tab[:, T_FREE:T_END], tabf[:, T_FREE:T_END]).then_inc(table_ready, 1)
            t.link(V.tensor_tensor(base, upto, n_tiles, ALU.subtract))
            t.close()
            m = Chain(dve, dve_m, 22, 0)
            m.link(V.scalar_tensor_tensor(base, base, float(P), cape[:, :], ALU.mult, ALU.subtract))
            m.link(V.tensor_tensor(ohm, oh_all[:, :, :, :].rearrange("p a t e -> p (a t) e"), experts(base, 2 * NT), ALU.mult))
            m.link(V.tensor_reduce(small[:, 0:2, :].rearrange("p a t -> p (a t)"), ohm, AX_X, ALU.add))
            m.link(V.tensor_tensor(slot_all[:, :, :], slot_all[:, :, :], small[:, 0:2, :].rearrange("p a t -> p t a"), ALU.add))
            first_low = small[:, 4, :]
            m.add(V.tensor_tensor(first_low, slot_all[:, :, 0], slot_all[:, :, 1], ALU.is_lt))
            m.add(V.tensor_tensor(small[:, 0, :], slot_all[:, :, 0], slot_all[:, :, 1], ALU.min))
            m.link(V.tensor_tensor(small[:, 1, :], slot_all[:, :, 0], slot_all[:, :, 1], ALU.max))
            m.link(V.tensor_copy(yrow_i[:, :, :], small[:, 0:2, :].rearrange("p a t -> p t a")))
            V.tensor_tensor(expo, lg_all[:, :, :], m_all[:, :].unsqueeze(2).broadcast_to([P, NT, E]),
                            ALU.subtract).then_inc(exp_in, 1)
            dve.wait_ge(exp_done, 1)
            m.link(V.tensor_reduce(small[:, 2, :], expo2, AX_X, ALU.add))
            m.link(V.reciprocal(small[:, 2, :], small[:, 2, :]))
            m.link(V.tensor_tensor(expo2, expo2, small[:, 2, :].unsqueeze(2).broadcast_to([P, NT, E]), ALU.mult))
            for n in range(2):
                m.link(V.tensor_tensor(expo, expo2, oh_all[:, n, :, :], ALU.mult))
                m.link(V.tensor_reduce(wmix[:, n, :], expo, AX_X, ALU.add))
            m.link(V.tensor_tensor(small[:, 3, :], wmix[:, 0, :], wmix[:, 1, :], ALU.add))
            m.link(V.reciprocal(small[:, 3, :], small[:, 3, :]))
            m.link(V.tensor_tensor(wmix[:, :, :], wmix[:, :, :], small[:, 3, :].unsqueeze(1).broadcast_to([P, 2, NT]),
                                   ALU.mult))
            m.link(V.tensor_scalar(small[:, 5, :], first_low, -1.0, 1.0, ALU.mult, ALU.add))
            m.link(V.tensor_tensor(small[:, 0:2, :], wmix[:, :, :], small[:, 4:6, :], ALU.mult))
            m.link(V.tensor_tensor(small[:, 2:4, :], wmix[:, :, :], small[:, 0:2, :], ALU.subtract))
            m.link(V.tensor_tensor(wmix[:, 0, :], small[:, 0, :], small[:, 1, :], ALU.add))
            V.tensor_tensor(wmix[:, 1, :], small[:, 2, :], small[:, 3, :], ALU.add).then_inc(mix_ready, 1)
            m.close()

            def low_rows(t):
                dve.wait_ge(rT_high, t + 1)
                V.tensor_tensor(rT[:, 1, :, :], ps_rT[:, :].rearrange("p (k c) -> p k c", c=P),
                                rT[:, 0, :, :].bitcast(F32), ALU.subtract).then_inc(rT_low, 1)

            def gate(t):
                dve.wait_ge(up_done, 2 * t + 2)
                dve.wait_ge(silu_done, t + 1)
                V.tensor_tensor(hid, ps_u[:, :], sg, ALU.mult).then_inc(hid_ready, 1)

            def low_hid(t):
                dve.wait_ge(hT_high, t + 1)
                V.tensor_tensor(hT[:, 1, :, :], ps_hT[:, :].rearrange("p (k c) -> p k c", c=P),
                                hT[:, 0, :, :].bitcast(F32), ALU.subtract).then_inc(hT_low, 1)

            low_rows(0)
            gate(0)
            low_rows(1)
            low_hid(0)

            def tile(t):
                gate(t)
                low_rows(t + 1)
                low_hid(t)

            tiles_ = table_value(dve, T_TILES, NFULL)
            with dve.Fori(1, NFULL) as t:
                tile(t)
            with dve.Fori(NFULL, NTILE) as t:
                with dve.If(t < tiles_):
                    tile(t)

            def mix(buf, i, s, which, done):
                xi = x1[:, ds(i, 1), :].rearrange("p a d -> p (a d)")
                V.scalar_tensor_tensor(xi, buf[:, ds(s, 1), :].rearrange("p a d -> p (a d)"), wmix[:, which, ds(i, 1)],
                                       xi, ALU.mult, ALU.add).then_inc(done, 1)

            dve.wait_ge(mix_ready, 1)
            dve.wait_ge(fetched_low, 16 * NT)
            for g, buf in enumerate(fetch_buf):
                with dve.Fori(0, FLIGHT) as s:
                    mix(buf, s + g * FLIGHT, s, 0, low_mixed)
            dve.wait_ge(low_mixed, NT)
            for g, buf in enumerate(fetch_buf):
                for s in range(FLIGHT):
                    dve.wait_ge(fetched_high[s], 16 * (g + 1))
                    mix(buf, g * FLIGHT + s, s, 1, row_ready)

        @block.tensor
        def _(pe):
            def transposes(b):
                for k in range(KC):
                    pe.wait_ge(ctx_ready, TB * (b + 1))
                    if b > 0:
                        pe.wait_ge(xT_low, TB * b)
                    for j in range(TB):
                        last = nc.tensor.transpose(ps_T[k][:, j * P:(j + 1) * P], ctxq[:, j, k * P:(k + 1) * P],
                                                   ident[:, :])
                    last.then_inc(cT_formed, 1)
                for j in range(TB):
                    pe.wait_ge(xq_ready, TB * b + j + 1)
                    pe.wait_ge(cT_low, KC * b + j + 1)
                    for k in range(KC):
                        last = nc.tensor.transpose(ps_T[j][:, k * P:(k + 1) * P], xq[:, j, k * P:(k + 1) * P],
                                                   ident[:, :])
                    last.then_inc(xT_formed, 1)

            def attention(b, j):
                pe.wait_ge(xT_low, TB * b + j + 1)
                if TB * b + j >= 2:
                    pe.wait_ge(x1_ready, TB * b + j - 1)
                n = 0
                for k in range(KC):
                    for xp, cp in ((0, 0), (0, 1), (1, 0)):
                        last = nc.tensor.matmul(ps_at[j % 2][:, :], xT[:, j, xp, k, :], cT[:, cp, k, :],
                                                start=(n == 0), stop=(n == 3 * KC - 1))
                        n += 1
                last.then_inc(attn_done, 1)

            def router(b, turned):
                def turn(j):
                    pe.wait_ge(y2_ready, TB * b + j + 1)
                    if j == 1:
                        pe.wait_ge(xT_low, TB * (turned + 1))
                    for k in range(KC):
                        last = nc.tensor.transpose(ps_yT[j % 2][:, k * P:(k + 1) * P], y2[b % 2][:, j, k * P:(k + 1) * P],
                                                   ident[:, :])
                    last.then_inc(yT_formed, 1)

                turn(0)
                for j in range(TB):
                    if j + 1 < TB:
                        turn(j + 1)
                    pe.wait_ge(yT_ready, TB * b + j + 1)
                    for k in range(KC):
                        last = nc.tensor.matmul(ps_small[:, j * E:(j + 1) * E], y2T[:, j % 2, k, :], wr[:, k, :],
                                                start=(k == 0), stop=(k == KC - 1))
                last.then_inc(logits_done, 1)

            def ranks(b):
                pe.wait_ge(chosen, b + 1)
                nc.tensor.matmul(ps_small[:, TB * E:2 * TB * E], before[:, :], selb[:, :, :].rearrange("p t e -> p (t e)"),
                                 start=True, stop=False)
                nc.tensor.matmul(ps_small[:, TB * E:2 * TB * E], ones[:, :], cum[:, 0:TB, :].rearrange("p t e -> p (t e)"),
                                 start=False, stop=True).then_inc(ranks_done, 1)

            pe.wait_ge(masks_ready, 2)
            pe.wait_ge(wr_loaded, 16)
            for b in range(B):
                transposes(b)
                if b >= 1 and b + 1 < B:
                    if b >= 2:
                        pe.wait_ge(slots_ready, b - 1)
                    router(b - 1, b)
                attention(b, 0)
                if b >= 1 and b + 1 < B:
                    ranks(b - 1)
                for j in range(1, TB):
                    attention(b, j)
            for b in (B - 2, B - 1):
                pe.wait_ge(slots_ready, b)
                router(b, B - 1)
                ranks(b)
            pe.wait_ge(slots_ready, B)
            nc.tensor.matmul(ps_small[:, 0:E], ones[:, :], cum[:, TB, :], start=True, stop=True).then_inc(counts_done, 1)

            def turn_rows(t):
                pe.wait_ge(rows_loaded, 16 * (t + 1))
                for k in range(KC):
                    last = nc.tensor.transpose(ps_rT[:, k * P:(k + 1) * P], rows[:, k * P:(k + 1) * P], ident[:, :])
                return last

            def expert_of(t):
                return pe.value_load(tab[0:1, ds(T_PAR + t, 1)], min_val=0, max_val=1)

            def gate_up(t):
                slot_ = expert_of(t)
                ready = pe.value_load(tab[0:1, ds(T_WREADY + t, 1)], min_val=1, max_val=E)
                pe.wait_ge(w_ready, ready)
                pe.wait_ge(rT_low, t + 1)
                for m, bank in ((0, ps_g), (1, ps_u)):
                    n = 0
                    for k in range(KC):
                        for xp, wp in ((0, 0), (0, 1), (1, 0)):
                            last = nc.tensor.matmul(bank[:, :], rT[:, xp, k, :], wsplit[:, ds(slot_, 1), m, wp, k, :],
                                                    start=(n == 0), stop=(n == 3 * KC - 1))
                            n += 1
                    last.then_inc(up_done, 1)

            def down(t, first=False):
                slot_ = expert_of(t)
                pe.wait_ge(hT_low, t + 1)
                if not first:
                    pe.wait_ge(yt_ready, t)
                n = 0
                for k in range(KC):
                    for hp, wp in ((0, 0), (0, 1), (1, 0)):
                        last = nc.tensor.matmul(ps_y[:, :], hT[:, hp, k, :], wsplit[:, ds(slot_, 1), 2, wp, k, :],
                                                start=(n == 0), stop=(n == 3 * KC - 1))
                        n += 1
                last.then_inc(tiles_done, 1)

            def turn_hid(t):
                pe.wait_ge(hid_ready, t + 1)
                for k in range(KC):
                    last = nc.tensor.transpose(ps_hT[:, k * P:(k + 1) * P], hid[:, k * P:(k + 1) * P], ident[:, :])
                last.then_inc(hT_formed, 1)

            pe.wait_ge(table_ready, 1)
            turn_rows(0).then_inc(rT_formed, 1)
            nc.tensor.matmul(ps_small[:, 0:E], ones[:, :], cum[:, TB, :], start=True, stop=True).then_inc(tiles_done, 1)
            gate_up(0)
            turn_rows(1).then_inc(rT_formed, 1)
            turn_hid(0)
            gate_up(1)
            pe.wait_ge(rT_low, 2)
            turn_rows(2).then_inc(rT_formed, 1)
            down(0, True)
            turn_hid(1)

            def tile(t):
                gate_up(t)
                turn_rows(t + 1).then_inc(rT_formed, 1)
                down(t - 1)
                turn_hid(t)

            tiles_ = table_value(pe, T_TILES, NFULL)
            with pe.Fori(2, NFULL) as t:
                tile(t)
            with pe.Fori(NFULL, NTILE) as t:
                with pe.If(t < tiles_):
                    tile(t)
            down(table_value(pe, T_LAST + 1, NFULL - 1, NTILE - 1))


_INS = ['x', 'ctx_2048', 'L0_ffn_Wr', 'L0_ffn_Wg', 'L0_ffn_Wu', 'L0_ffn_Wd']
_OUTS = [((4, 512, 512), 'float32')]


def kernel(**inputs):
    import numpy as _np
    import concourse.bacc as _bacc
    from concourse import mybir as _mybir
    from concourse.bass_utils import run_bass_kernel_spmd as _run

    nc = _bacc.Bacc("TRN2", target_bir_lowering=False, num_devices=1)
    arrays, args = {}, []
    for name in _INS:
        a = _np.ascontiguousarray(inputs[name])
        arrays[f"in_{name}_dram"] = a
        args.append(nc.dram_tensor(f"in_{name}_dram", a.shape, _mybir.dt.from_np(a.dtype), kind="ExternalInput").ap())
    for i, (shape, dtype) in enumerate(_OUTS):
        dt = _mybir.dt.from_np(_np.dtype(dtype))
        args.append(nc.dram_tensor(f"out_{i}_dram", shape, dt, kind="ExternalOutput").ap())
    xattn_moe(nc, *args)
    r = _run(nc, [arrays], core_ids=[0])
    return r.results[0]["out_0_dram"]
```

```python
from contextlib import ExitStack

import concourse.bass as bass
from concourse import mybir

F32 = mybir.dt.float32
F32R = mybir.dt.float32r
BF16 = mybir.dt.bfloat16
I32 = mybir.dt.int32
U32 = mybir.dt.uint32
ALU = mybir.AluOpType
ACT = mybir.ActivationFunctionType
AX_X = mybir.AxisListType.X
ds = bass.ds

P = 128
B, S, D = 4, 512, 512
E, F, TOPK = 8, 512, 2
KC = D // P
TB = S // P
NT = B * TB
HB = TB // 2
LN_EPS = 1e-5
FP8_MAX, ACT_EPS, W_EPS = 448.0, 1e-4, 1e-6

CAP = B * S + P
ZROW = E * CAP
NTILE = (TOPK * B * S + E * (P - 1)) // P
NFULL = TOPK * B * S // P
WARM_UP = 14
FLIGHT = 8
T_PAR, T_WREADY, T_ROW, T_PAD, T_FREE, T_LAST, T_LOW, T_TILES, T_END = 0, 40, 80, 120, 128, 136, 138, 139, 140

EXP_MASK = 0x7F800000
MIN_NORMAL = 2.0 ** -6
ROUND_AT = 1.5 * 2.0 ** 20


class Chain:

    def __init__(self, eng, sem, per, i, before=0):
        self.eng, self.sem, self.per, self.start, self.n = eng, sem, per, before + i * per, 0

    def add(self, ins):
        ins.then_inc(self.sem, 1)
        self.n += 1

    def sync(self):
        self.eng.wait_ge(self.sem, self.start + self.n)

    def link(self, ins):
        self.add(ins)
        self.sync()

    def close(self):
        assert self.n == self.per, (self.n, self.per)


def xattn_moe(nc, x, ctx_in, Wr, Wg, Wu, Wd, out):
    with ExitStack() as ctx:
        def sb(name, shape, dt):
            return ctx.enter_context(nc.sbuf_tensor(name, shape, dt))

        def sem(name):
            return ctx.enter_context(nc.semaphore(name))

        x1 = sb("x1", [P, NT, D], F32)
        wsplit = sb("wsplit", [P, 2, 3, 2, KC, F], F32R)
        wraw = sb("wraw", [P, 2, KC, F], F32)
        cxq = sb("cxq", [P, 2 * TB, D], F32)
        ctxq = cxq[:, 0:TB, :]
        xq = cxq[:, TB:2 * TB, :]
        magx = sb("magx", [P, 2, D], F32)
        magc = sb("magc", [P, 2, D], F32)
        y2_even = sb("y2_even", [P, TB, D], F32)
        y2T = sb("y2T", [P, 2, KC, P], F32)
        xT = sb("xT", [P, TB, 2, KC, P], F32R)
        wr = sb("wr", [P, KC, E], F32)
        ident = sb("ident", [P, P], F32)
        before = sb("before", [P, P], BF16)
        ones = sb("ones", [P, P], BF16)
        iot = sb("iot", [P, 64], I32)
        alti = sb("alti", [P, E], I32)
        io = sb("io", [P, 64], F32)
        alt = sb("alt", [P, E], F32)
        rev = sb("rev", [P, E], F32)
        cape = sb("cape", [P, E], F32)
        eps = sb("eps", [P, 1], F32)
        table_pull = sb("table_pull", [P, 1], F32)
        stats = sb("stats", [P, 2, TB, 6], F32)
        mv = sb("mv", [P, 2, TB, 2], F32)
        sd = sb("sd", [P, 2, TB], F32)
        rstd = sb("rstd", [P, 2, TB], F32)
        nmr = sb("nmr", [P, 2, TB], F32)
        NB = TB * KC
        xmax = sb("xmax", [P, NB], F32)
        xsc = sb("xsc", [P, NB], F32)
        xinv = sb("xinv", [P, NB], F32)
        cmaxp = sb("cmaxp", [P, NB], F32)
        cmax = sb("cmax", [P, NB], F32)
        csc = sb("csc", [P, NB], F32)
        cinv = sb("cinv", [P, NB], F32)
        rl = sb("rl", [P, TB, E], F32)
        rl2 = sb("rl2", [P, TB, E], F32)
        eq = sb("eq", [P, TB, E], F32)
        top = sb("top", [P, 2, TB], F32)
        pick = sb("pick", [P, 2, TB], F32)
        oh = sb("oh", [P, 2, TB, E], F32)
        selb = sb("selb", [P, TB, E], BF16)
        cum = sb("cum", [P, TB + 1, E], BF16)
        place = sb("place", [P, TB, E], F32)
        slot = sb("slot", [P, TB, 2], F32)
        slot_i = sb("slot_i", [P, 2, TB, 2], I32)
        oh_all = sb("oh_all", [P, 2, NT, E], F32)
        slot_all = sb("slot_all", [P, NT, 2], F32)
        lg_all = sb("lg_all", [P, NT, E], F32)
        m_all = sb("m_all", [P, NT], F32)
        yrow_i = sb("yrow_i", [P, NT, 2], I32)
        wmix = sb("wmix", [P, 2, NT], F32)
        count = sb("count", [P, 4, E], F32)
        tabf = sb("tabf", [P, T_END], F32)
        tab = sb("tab", [P, T_END], I32)
        small = sb("small", [P, 6, NT], F32)

        cT = wsplit[:, 1, 0, :, :, :]
        y2 = (y2_even, wraw[:, 1, :, :])
        rows, hid = magx[:, 0, :], magx[:, 1, :]
        sg, yt = magc[:, 0, :], magc[:, 1, :]
        rT, hT = xT[:, 0, :, :, :], xT[:, 1, :, :, :]
        zero = xq[:, 0, :]
        blank = wsplit[:, 0, 2, 1, 0, :].bitcast(F32)
        fetch_buf = (wraw[:, :, :, :].rearrange("p s k f -> p (s k) f"), cxq)
        spare = ctxq[:, :, :].rearrange("p t d -> p (t d)")
        le = spare[:, 0:NTILE * E].rearrange("p (t e) -> p t e", e=E)
        le2 = spare[:, 512:512 + NTILE * E].rearrange("p (t e) -> p t e", e=E)
        over = spare[:, 1024:1024 + E * NT].rearrange("p (e j) -> p e j", j=NT)
        expo = spare[:, 1152:1152 + NT * E].rearrange("p (t e) -> p t e", e=E)
        expo2 = spare[:, 1280:1280 + NT * E].rearrange("p (t e) -> p t e", e=E)
        ohm = spare[:, 1408:1408 + 2 * NT * E].rearrange("p (a e) -> p a e", e=E)

        ps = [ctx.enter_context(nc.psum_tensor(f"ps{i}", [P, 512], F32)) for i in range(8)]
        ps_T, ps_at, ps_small = ps[0:4], ps[4:6], ps[7]
        ps_g, ps_u, ps_y, ps_hT, ps_rT = ps[0], ps[1], ps[4], ps[5], ps[2]

        def logits_needed(b, lo):
            return b + 1 + (lo > 0)

        def turned_in(j):
            return (ps[6], ps_at[0], ps[6], ps_T[3])[j]

        def choice_bank(b, lo):
            return ps_small if b + 1 < B else ps_T[1 + lo // HB]

        grouped = nc.dram_tensor("grouped", [ZROW + P, D], F32, kind="Internal").ap()
        results = nc.dram_tensor("results", [NTILE * P, D], F32, kind="Internal").ap()

        x_rows = x.rearrange("b s d -> (b s) d")
        out_rows = out.rearrange("b s d -> (b s) d")
        weights = (Wg, Wu, Wd)

        x_loaded, ctx_loaded, wr_loaded = sem("x_loaded"), sem("ctx_loaded"), sem("wr_loaded")
        masks_ready, consts_ready, pool_set = sem("masks_ready"), sem("consts_ready"), sem("pool_set")
        const_steps = sem("const_steps")
        ctx_maxed, ctx_max_all, ctx_scaled = sem("ctx_maxed"), sem("ctx_max_all"), sem("ctx_scaled")
        x_scaled, ctx_quant = sem("x_scaled"), sem("ctx_quant")
        x_quant, x_quant_pool = sem("x_quant"), sem("x_quant_pool")
        ln1_var, ln1_sd, ln1_ready, ln1_done = sem("ln1_var"), sem("ln1_sd"), sem("ln1_ready"), sem("ln1_done")
        ctx_magnified, ctx_biased, ctx_rounded, ctx_ready = sem("ctx_magnified"), sem("ctx_biased"), sem("ctx_rounded"), sem("ctx_ready")
        x_biased, x_rounded, xq_ready = sem("x_biased"), sem("x_rounded"), sem("xq_ready")
        cT_formed, cT_high, cT_low = sem("cT_formed"), sem("cT_high"), sem("cT_low")
        xT_formed, xT_high, xT_low = sem("xT_formed"), sem("xT_high"), sem("xT_low")
        attn_done, x1_ready, x1_stats = sem("attn_done"), sem("x1_ready"), sem("x1_stats")
        ln2_var, ln2_sd, ln2_ready, y2_ready = sem("ln2_var"), sem("ln2_sd"), sem("ln2_ready"), sem("y2_ready")
        yT_formed, yT_ready, logits_done = sem("yT_formed"), sem("yT_ready"), sem("logits_done")
        chosen, ranks_done, slots_ready = sem("chosen"), sem("ranks_done"), sem("slots_ready")
        scattered = (sem("scattered_even"), sem("scattered_odd"))
        w_loaded = [sem("w_loaded0"), sem("w_loaded1")]
        w_split, w_ready = sem("w_split"), sem("w_ready")
        counts_done, pads_ready = sem("counts_done"), sem("pads_ready")
        table_ready, zero_ready = sem("table_ready"), sem("zero_ready")
        padded, rows_loaded = sem("padded"), sem("rows_loaded")
        rT_formed, rT_high, rT_low = sem("rT_formed"), sem("rT_high"), sem("rT_low")
        up_done, silu_done, hid_ready = sem("up_done"), sem("silu_done"), sem("hid_ready")
        hT_formed, hT_high, hT_low = sem("hT_formed"), sem("hT_high"), sem("hT_low")
        tiles_done, yt_ready, yt_stored = sem("tiles_done"), sem("yt_ready"), sem("yt_stored")
        exp_in, exp_done, mix_ready = sem("exp_in"), sem("exp_done"), sem("mix_ready")
        fetched_low = sem("fetched_low")
        fetched_high = [sem(f"fetched_high{s}") for s in range(FLIGHT)]
        low_mixed, row_ready, out_stored = sem("low_mixed"), sem("row_ready"), sem("out_stored")
        results_cleared = sem("results_cleared")
        waited = sem("waited")
        ln1_steps, quant_steps, ln2_steps = sem("ln1_steps"), sem("quant_steps"), sem("ln2_steps")
        choice_steps, table_steps, mix_steps = sem("choice_steps"), sem("table_steps"), sem("mix_steps")

        def wait_alone(eng, sem_, value):
            eng.wait_ge(sem_, value)
            eng.sem_inc(waited, 1)

        def table_value(eng, column, low, high=NTILE):
            return eng.value_load(tab[0:1, column:column + 1], min_val=low, max_val=high)

        def pad_expert(eng, e):
            pad = eng.value_load(tab[0:1, T_PAD + e:T_PAD + e + 1], min_val=0, max_val=ZROW - P)
            eng.dma_start(grouped[ds(pad, P), :], zero).then_inc(padded, 16)

        block = ctx.enter_context(nc.Block())

        @block.sync
        def _(sp):
            def load_x(b):
                sp.dma_start(x1[:, TB * b:TB * b + TB, :],
                             x_rows[S * b:S * b + S, :].rearrange("(t p) d -> p t d", p=P)).then_inc(x_loaded, 16)

            def load_ctx(b):
                sp.dma_start(ctxq[:, :, :], ctx_in[b].rearrange("(t p) d -> p t d", p=P)).then_inc(ctx_loaded, 16)

            load_ctx(0)
            load_x(0)
            sp.dma_start(wr[:, :, :], Wr.rearrange("(k p) e -> p k e", p=P)).then_inc(wr_loaded, 16)
            for b in range(1, B):
                sp.wait_ge(x_loaded, 16 * b)
                load_x(b)
            for b in range(1, B):
                sp.wait_ge(cT_formed, TB * b)
                load_ctx(b)
                sp.wait_ge(consts_ready, 1)
                part = NTILE // (B - 1)
                assert part * (B - 1) == NTILE
                sp.dma_start(results[(b - 1) * part * P:b * part * P, :].rearrange("(t p) d -> p t d", p=P),
                             blank.unsqueeze(1).broadcast_to([P, part, D])).then_inc(results_cleared, 16)

            sp.wait_ge(zero_ready, 1)
            sp.dma_start(grouped[ZROW:ZROW + P, :], zero).then_inc(padded, 16)
            sp.wait_ge(pads_ready, 1)
            for e in range(E // 2):
                pad_expert(sp, e)
            sp.wait_ge(padded, 16 * (E + 1))
            sp.wait_ge(table_ready, 1)
            sp.wait_ge(scattered[0], 16 * NT)
            sp.wait_ge(scattered[1], 16 * NT)

            def load_rows(t):
                row = sp.value_load(tab[0:1, ds(T_ROW + t, 1)], min_val=0, max_val=ZROW)
                sp.dma_start(rows, grouped[ds(row, P), :]).then_inc(rows_loaded, 16)

            def store_result(t):
                sp.wait_ge(yt_ready, t + 1)
                sp.dma_start(results[ds(t * P, P), :], yt).then_inc(yt_stored, 16)

            load_rows(0)
            sp.wait_ge(rT_formed, 1)
            load_rows(1)
            sp.wait_ge(rT_formed, 2)
            load_rows(2)
            sp.wait_ge(results_cleared, 16 * (B - 1))

            def rows_and_result(t):
                sp.wait_ge(rT_formed, t + 2)
                load_rows(t + 2)
                store_result(t - 1)

            tiles_ = table_value(sp, T_TILES, NFULL)
            with sp.Fori(1, NFULL - 1) as t:
                rows_and_result(t)
            with sp.Fori(NFULL - 1, NTILE - 1) as t:
                with sp.If(t + 1 < tiles_):
                    rows_and_result(t)
            store_result(table_value(sp, T_LAST, NFULL - 2, NTILE - 2))
            store_result(table_value(sp, T_LAST + 1, NFULL - 1, NTILE - 1))

            with sp.Fori(0, NT) as i:
                sp.wait_ge(row_ready, i + 1)
                sp.dma_start(out_rows[ds(i * P, P), :],
                             x1[:, ds(i, 1), :].rearrange("p a d -> p (a d)")).then_inc(out_stored, 16)
            sp.wait_ge(out_stored, 16 * NT)

        @block.gpsimd
        def _(pool):
            nc.gpsimd.memset(ident[:, :], 0.0).then_inc(pool_set, 1)
            nc.gpsimd.memset(before[:, :], 1.0).then_inc(pool_set, 1)
            nc.gpsimd.memset(ones[:, :], 1.0).then_inc(pool_set, 1)
            nc.gpsimd.iota(iot[:, :], pattern=[[1, 64]], base=0, channel_multiplier=0).then_inc(pool_set, 1)
            nc.gpsimd.iota(alti[:, :], pattern=[[0, E // 2], [-2, 2]], base=1, channel_multiplier=0).then_inc(pool_set, 1)
            pool.wait_ge(pool_set, 5)
            nc.gpsimd.affine_select(out=ident[:, :], in_=ident[:, :], compare_op=ALU.not_equal, fill=1.0,
                                    base=0, pattern=[[-1, P]], channel_multiplier=1).then_inc(masks_ready, 1)
            nc.gpsimd.affine_select(out=before[:, :], in_=before[:, :], compare_op=ALU.is_gt, fill=0.0,
                                    base=0, pattern=[[1, P]], channel_multiplier=-1).then_inc(masks_ready, 1)

            def load_weights(e, m, stage):
                src = weights[m][ds(e, 1)].rearrange("a (k p) f -> p (a k) f", p=P)
                pool.dma_start(wraw[:, stage, :, :], src).then_inc(w_loaded[stage], 16)

            def split_weights(m, slot_, stage, nth, count_before, last):
                wait_alone(pool, w_loaded[stage], 16 * (nth + 1))
                high, low = wsplit[:, slot_, m, 0, :, :], wsplit[:, slot_, m, 1, :, :]
                nc.gpsimd.tensor_scalar(high, wraw[:, stage, :, :], 1.0, 1.0, ALU.mult, ALU.mult).then_inc(w_split, 1)
                pool.wait_ge(w_split, count_before + 1)
                nc.gpsimd.tensor_tensor(low, wraw[:, stage, :, :], high.bitcast(F32),
                                        ALU.subtract).then_inc(w_split if last is None else w_ready, 1)
                if last is None:
                    wait_alone(pool, w_split, count_before + 2)
                else:
                    wait_alone(pool, w_ready, last)

            def ctx_max(b):
                pool.wait_ge(ctx_maxed, b + 1)
                nc.gpsimd.partition_all_reduce(cmax[:, :], cmaxp[:, :], P,
                                               bass.bass_isa.ReduceOp.max).then_inc(ctx_max_all, 1)

            def round_off(b, j, buf, mag, biased, rounded):
                pool.wait_ge(biased, TB * b + j + 1)
                nc.gpsimd.tensor_tensor(buf[:, j, :], buf[:, j, :], mag[:, j % 2, :], ALU.subtract).then_inc(rounded, 1)

            def ctx_bias(b, j):
                pool.wait_ge(ctx_magnified, TB * (b - 1) + j + 1)
                nc.gpsimd.tensor_tensor(ctxq[:, j, :], ctxq[:, j, :], magc[:, j % 2, :], ALU.add).then_inc(ctx_biased, 1)

            def quantise_x(j):
                pool.wait_ge(x_scaled, 1)
                for k in range(KC):
                    v = xq[:, j, k * P:(k + 1) * P]
                    last = nc.gpsimd.tensor_scalar(v, v, xinv[:, KC * j + k:KC * j + k + 1], 1.0, ALU.mult, ALU.mult)
                last.then_inc(x_quant_pool, 1)

            def quantisation(b):
                ctx_max(b)
                for j in range(TB):
                    if b > 0:
                        ctx_bias(b, j)
                    round_off(b, j, ctxq, magc, ctx_biased, ctx_rounded)
                    if b == 0 and j in (1, 2):
                        quantise_x(HB + j - 1)
                for j in range(TB):
                    round_off(b, j, xq, magx, x_biased, x_rounded)

            def scatter(b, lo=0, n=TB):
                pool.wait_ge(slots_ready, b + 1 + (lo > 0))
                for j in range(lo, lo + n):
                    for c in range(2):
                        nc.gpsimd.indirect_dma_start(
                            grouped[:, :], bass.IndirectOffsetOnAxis(ap=slot_i[:, b % 2, j, c:c + 1], axis=0),
                            y2[b % 2][:, j, :], None).then_inc(scattered[b % 2], 16)

            load_weights(0, 0, 0)
            quantisation(0)
            split_weights(0, 0, 0, 0, 0, None)
            load_weights(0, 1, 0)
            quantisation(1)
            split_weights(1, 0, 0, 1, 2, None)
            load_weights(0, 2, 0)
            quantisation(2)
            scatter(0)
            quantisation(3)
            scatter(1)
            pool.wait_ge(results_cleared, 16 * (B - 1))
            split_weights(2, 0, 0, 2, 4, 1)
            load_weights(1, 0, 0)
            scatter(2)
            scatter(3, 0, HB)
            scatter(3, HB, HB)
            pool.wait_ge(attn_done, NT)
            split_weights(0, 1, 0, 3, 5, None)
            pool.wait_ge(rows_loaded, 48)
            load_weights(1, 2, 0)
            pool.wait_ge(scattered[1], 16 * NT)
            load_weights(1, 1, 1)
            split_weights(1, 1, 1, 0, 7, None)
            load_weights(2, 0, 1)
            split_weights(2, 1, 0, 4, 9, 2)
            load_weights(2, 1, 0)
            pool.wait_ge(table_ready, 1)

            def expert(e, slot_, nth0, nth1, before_, first_stage, load_next):
                free = pool.value_load(tab[0:1, ds(T_FREE + e - 2, 1)], min_val=1, max_val=NTILE + 1)
                wait_alone(pool, tiles_done, free)
                a, z = first_stage, 1 - first_stage
                n = [nth0, nth1]
                split_weights(0, slot_, a, n[a], before_, None)
                load_weights(e, 2, a)
                split_weights(1, slot_, z, n[z], before_ + 2, None)
                if load_next:
                    load_weights(e + 1, 0, z)
                split_weights(2, slot_, a, n[a] + 1, before_ + 4, e + 1)
                if load_next:
                    load_weights(e + 1, 1, a)

            with pool.Fori(0, E // 2 - 2) as q:
                expert(2 + 2 * q, 0, 5 + 3 * q, 1 + 3 * q, 10 + 10 * q, 1, True)
                expert(3 + 2 * q, 1, 6 + 3 * q, 3 + 3 * q, 15 + 10 * q, 0, True)
            expert(E - 2, 0, 11, 7, 30, 1, True)
            expert(E - 1, 1, 12, 9, 35, 0, False)

            def fetch(i, which, fetched):
                nc.gpsimd.indirect_dma_start(
                    fetch_buf[i // FLIGHT][:, i % FLIGHT, :], None, results[:, :],
                    bass.IndirectOffsetOnAxis(ap=yrow_i[:, i, which:which + 1], axis=0)).then_inc(fetched, 16)

            pool.wait_ge(mix_ready, 1)
            wait_alone(pool, yt_stored, table_value(pool, T_LOW, NFULL // 2) * 16)
            for i in range(NT):
                fetch(i, 0, fetched_low)
            wait_alone(pool, yt_stored, table_value(pool, T_TILES, NFULL) * 16)
            for i in range(NT):
                pool.wait_ge(low_mixed, i + 1)
                if i >= FLIGHT:
                    pool.wait_ge(row_ready, i - FLIGHT + 1)
                fetch(i, 1, fetched_high[i % FLIGHT])

        @block.scalar
        def _(act):
            def ln1_deviation(b):
                act.wait_ge(ln1_var, b + 1)
                nc.scalar.activation(sd[:, 0, :], mv[:, 0, :, 1], ACT.Sqrt, bias=eps[:, :]).then_inc(ln1_sd, 1)

            def normalise(which, x_tile, j, out_, done):
                nc.scalar.activation(out_[:, j, :], x1[:, x_tile, :], ACT.Identity, bias=nmr[:, which, j:j + 1],
                                     scale=rstd[:, which, j:j + 1]).then_inc(done, 1)

            def ln1(b):
                act.wait_ge(ln1_ready, b + 1)
                if b > 0:
                    act.wait_ge(xT_formed, TB * b)
                for j in range(TB):
                    normalise(0, TB * b + j, j, xq, ln1_done)

            def ln2(b, half):
                act.wait_ge(ln2_ready, 2 * b + half + 1)
                if b >= 2 and half == 0:
                    act.wait_ge(scattered[b % 2], 32 * TB * (b // 2))
                for j in range(HB * half, HB * half + HB):
                    normalise(1, TB * b + j, j, y2[b % 2], y2_ready)

            def ln2_deviation(b, half):
                act.wait_ge(ln2_var, 2 * b + half + 1)
                nc.scalar.activation(sd[:, 1, HB * half:HB * half + HB], mv[:, 1, HB * half:HB * half + HB, 1],
                                     ACT.Sqrt, bias=eps[:, :]).then_inc(ln2_sd, 1)

            def scale_blocks(b, j, buf, factors, before_, count_before_, after_):
                act.wait_ge(before_, count_before_)
                for k in range(KC):
                    v = buf[:, j, k * P:(k + 1) * P]
                    last = nc.scalar.activation(v, v, ACT.Copy, scale=factors[:, KC * j + k:KC * j + k + 1])
                last.then_inc(after_, 1)

            def quantise_ctx(b, j):
                scale_blocks(b, j, ctxq, cinv, ctx_scaled, b + 1, ctx_quant)

            def quantise_x(b, j):
                scale_blocks(b, j, xq, xinv, x_scaled, b + 1, x_quant)

            def dequantise_ctx(b, j):
                scale_blocks(b, j, ctxq, csc, ctx_rounded, TB * b + j + 1, ctx_ready)

            def dequantise_x(b, j):
                scale_blocks(b, j, xq, xsc, x_rounded, TB * b + j + 1, xq_ready)

            def high_ctx(b):
                for k in range(KC):
                    act.wait_ge(cT_formed, KC * b + k + 1)
                    nc.scalar.activation(cT[:, 0, k, :], ps_T[k][:, :], ACT.Copy).then_inc(cT_high, 1)

            def high_x(b, j):
                act.wait_ge(xT_formed, TB * b + j + 1)
                nc.scalar.activation(xT[:, j, 0, :, :], ps_T[j][:, :].rearrange("p (k c) -> p k c", c=P),
                                     ACT.Copy).then_inc(xT_high, 1)

            def transposed_y2(b, j):
                act.wait_ge(yT_formed, TB * b + j + 1)
                nc.scalar.activation(y2T[:, j % 2, :, :], turned_in(j)[:, :].rearrange("p (k c) -> p k c", c=P),
                                     ACT.Copy).then_inc(yT_ready, 1)

            act.wait_ge(consts_ready, 1)
            nc.scalar.activation(table_pull[:, :], eps[:, :], ACT.Sqrt)
            ln1_deviation(0)
            quantise_ctx(0, 0)
            ln1(0)
            quantise_ctx(0, 1)
            quantise_ctx(0, 2)
            quantise_ctx(0, 3)
            ln1_deviation(1)
            for j in range(HB):
                quantise_x(0, j)
            for j in range(TB):
                dequantise_ctx(0, j)
            dequantise_x(0, 0)
            dequantise_x(0, 1)
            high_ctx(0)
            dequantise_x(0, 2)
            high_x(0, 0)
            high_x(0, 1)
            dequantise_x(0, 3)
            high_x(0, 2)
            high_x(0, 3)
            for b in range(B):
                if b + 1 < B:
                    ln1(b + 1)
                if b + 2 < B:
                    ln1_deviation(b + 2)
                if b >= 1:
                    ln2(b - 1, 1)
                if b + 1 < B:
                    quantise_ctx(b + 1, 0)
                    quantise_ctx(b + 1, 1)
                for j in range(HB, TB):
                    if b >= 1:
                        transposed_y2(b - 1, j)
                    if b + 1 < B:
                        quantise_ctx(b + 1, j)
                        quantise_x(b + 1, j - HB)
                if b + 1 < B:
                    quantise_x(b + 1, 2)
                    dequantise_ctx(b + 1, 0)
                    dequantise_ctx(b + 1, 1)
                    quantise_x(b + 1, 3)
                    dequantise_ctx(b + 1, 2)
                    dequantise_ctx(b + 1, 3)
                    dequantise_x(b + 1, 0)
                    ln2_deviation(b, 0)
                    dequantise_x(b + 1, 1)
                    ln2(b, 0)
                    high_ctx(b + 1)
                    dequantise_x(b + 1, 2)
                    high_x(b + 1, 0)
                    high_x(b + 1, 1)
                    ln2_deviation(b, 1)
                    for j in range(HB):
                        transposed_y2(b, j)
                    dequantise_x(b + 1, 3)
                    high_x(b + 1, 2)
                    high_x(b + 1, 3)
            ln2_deviation(B - 1, 0)
            ln2(B - 1, 0)
            ln2_deviation(B - 1, 1)
            for j in range(HB):
                transposed_y2(B - 1, j)
            ln2(B - 1, 1)
            for j in range(HB, TB):
                transposed_y2(B - 1, j)

            act.wait_ge(pads_ready, 1)
            for e in range(E // 2, E):
                pad_expert(act, e)

            act.wait_ge(exp_in, 1)
            nc.scalar.activation(expo2, expo, ACT.Exp).then_inc(exp_done, 1)

            def high_rows(t):
                act.wait_ge(rT_formed, t + 1)
                nc.scalar.activation(rT[:, 0, :, :], ps_rT[:, :].rearrange("p (k c) -> p k c", c=P),
                                     ACT.Copy).then_inc(rT_high, 1)

            def silu(t):
                act.wait_ge(up_done, 2 * t + 1)
                nc.scalar.activation(sg, ps_g[:, :], ACT.Silu).then_inc(silu_done, 1)

            def high_hid(t):
                act.wait_ge(hT_formed, t + 1)
                nc.scalar.activation(hT[:, 0, :, :], ps_hT[:, :].rearrange("p (k c) -> p k c", c=P),
                                     ACT.Copy).then_inc(hT_high, 1)

            def result(t, first=False):
                act.wait_ge(tiles_done, t + 2)
                if not first:
                    act.wait_ge(yt_stored, 16 * t)
                nc.scalar.activation(yt, ps_y[:, :], ACT.Copy).then_inc(yt_ready, 1)

            high_rows(0)
            silu(0)
            high_rows(1)
            high_hid(0)
            silu(1)
            high_rows(2)
            result(0, True)
            high_hid(1)

            def tile(t):
                act.wait_ge(hid_ready, t)
                silu(t)
                high_rows(t + 1)
                result(t - 1)
                high_hid(t)

            tiles_ = table_value(act, T_TILES, NFULL)
            with act.Fori(2, NFULL) as t:
                tile(t)
            with act.Fori(NFULL, NTILE) as t:
                with act.If(t < tiles_):
                    tile(t)
            result(table_value(act, T_LAST + 1, NFULL - 1, NTILE - 1))

        @block.vector
        def _(dve):
            V = nc.vector
            dve.wait_ge(masks_ready, 2)
            c = Chain(dve, const_steps, 6, 0)
            c.add(V.tensor_copy(io[:, :], iot[:, :]))
            c.add(V.tensor_copy(alt[:, :], alti[:, :]))
            c.add(V.memset(eps[:, :], LN_EPS))
            c.add(V.memset(cum[:, TB, :], 0.0))
            c.sync()
            c.add(V.tensor_scalar(rev[:, :], io[:, 0:E], -1.0, float(E), ALU.mult, ALU.add))
            c.add(V.tensor_scalar(cape[:, :], io[:, 0:E], float(CAP), None, ALU.mult))
            c.close()
            c.sync()
            V.memset(blank, 0.0).then_inc(consts_ready, 1)

            def tiles(ap, n=TB):
                return ap.unsqueeze(2).broadcast_to([P, n, E])

            def experts(ap, n=TB):
                return ap.unsqueeze(1).broadcast_to([P, n, E])

            def block_max(out_, buf):
                return V.tensor_reduce(out_[:, :], buf[:, :, :].rearrange("p t (k c) -> p (t k) c", c=P), AX_X, ALU.max,
                                       apply_absolute_value=True)

            def ln_aggregate(c, which, lo, n, var_ready):
                for j in range(lo, lo + n):
                    last = V.bn_aggr(mv[:, which, j, :], stats[:, which, j, :])
                    if j < lo + n - 1:
                        c.add(last)
                last.then_inc(var_ready, 1)

            def ln_scale(c, which, lo, n, ready):
                r_ = rstd[:, which, lo:lo + n]
                c.link(V.reciprocal(r_, sd[:, which, lo:lo + n]))
                V.scalar_tensor_tensor(nmr[:, which, lo:lo + n], mv[:, which, lo:lo + n, 0], -1.0, r_,
                                       ALU.mult, ALU.mult).then_inc(ready, 1)

            def ln2_aggregate(c, b, half):
                dve.wait_ge(x1_stats, TB * b + HB * half + HB)
                ln_aggregate(c, 1, HB * half, HB, ln2_var)

            def ln1_scale(c, b):
                dve.wait_ge(ln1_sd, b + 1)
                ln_scale(c, 0, 0, TB, ln1_ready)
                c.close()

            def ln2_scale(c, b, half):
                dve.wait_ge(ln2_sd, 2 * b + half + 1)
                ln_scale(c, 1, HB * half, HB, ln2_ready)

            def scales(c, maxima, scale, inv, floor, ready):
                c.link(V.tensor_scalar(maxima[:, :], maxima[:, :], floor, None, ALU.max))
                c.add(V.tensor_scalar(scale[:, :], maxima[:, :], 1.0 / FP8_MAX, None, ALU.mult))
                c.link(V.reciprocal(inv[:, :], maxima[:, :]))
                V.tensor_scalar(inv[:, :], inv[:, :], FP8_MAX, None, ALU.mult).then_inc(ready, 1)

            def ln1_stats(c, b):
                dve.wait_ge(x_loaded, 16 * (b + 1))
                for j in range(TB):
                    c.add(V.bn_stats(stats[:, 0, j, :], x1[:, TB * b + j, :]))
                c.sync()
                ln_aggregate(c, 0, 0, TB, ln1_var)

            def ctx_maxima(b):
                dve.wait_ge(ctx_loaded, 16 * (b + 1))
                block_max(cmaxp, ctxq).then_inc(ctx_maxed, 1)

            def x_maxima(c, b):
                dve.wait_ge(ln1_done, TB * (b + 1))
                c.link(block_max(xmax, xq))

            def ctx_scales(c, b):
                dve.wait_ge(ctx_max_all, b + 1)
                scales(c, cmax, csc, cinv, W_EPS, ctx_scaled)

            def to_grid(c, b, j, buf, mag, quantised, rounded, biased):
                v, m = buf[:, j, :], mag[:, j % 2, :]
                dve.wait_ge(*quantised)
                if TB * b + j >= 2:
                    dve.wait_ge(rounded, TB * b + j - 1)
                c.link(V.tensor_scalar(m.bitcast(U32), v.bitcast(U32), EXP_MASK, None, ALU.bitwise_and))
                c.link(V.tensor_scalar(m, m, MIN_NORMAL, ROUND_AT, ALU.max, ALU.mult))
                V.tensor_tensor(v, v, m, ALU.add).then_inc(biased, 1)

            def ctx_magnitude(c, b, j):
                dve.wait_ge(ctx_quant, TB * b + j + 1)
                dve.wait_ge(ctx_rounded, TB * b + j - 1)
                m = magc[:, j % 2, :]
                c.link(V.tensor_scalar(m.bitcast(U32), ctxq[:, j, :].bitcast(U32), EXP_MASK, None, ALU.bitwise_and))
                V.tensor_scalar(m, m, MIN_NORMAL, ROUND_AT, ALU.max, ALU.mult).then_inc(ctx_magnified, 1)

            def ctx_to_grid(c, b, j):
                to_grid(c, b, j, ctxq, magc, (ctx_quant, TB * b + j + 1), ctx_rounded, ctx_biased)

            def x_to_grid(c, b, j):
                if b == 0 and j >= HB:
                    quantised = x_quant_pool, j - HB + 1
                else:
                    quantised = x_quant, TB * b + j + 1 - (HB if b > 0 else 0)
                to_grid(c, b, j, xq, magx, quantised, x_rounded, x_biased)

            NL1, NL2, NQ0, NQ = TB + 3 + 1, 2 + 2, 1 + 3 + 3 + 2 * 2 * TB, 1 + 3 + 3 + 3 * TB

            def low_ctx(b):
                for k in range(KC):
                    dve.wait_ge(cT_high, KC * b + k + 1)
                    V.tensor_tensor(cT[:, 1, k, :], ps_T[k][:, :], cT[:, 0, k, :].bitcast(F32),
                                    ALU.subtract).then_inc(cT_low, 1)

            def low_x(b, j):
                dve.wait_ge(xT_high, TB * b + j + 1)
                V.tensor_tensor(xT[:, j, 1, :, :], ps_T[j][:, :].rearrange("p (k c) -> p k c", c=P),
                                xT[:, j, 0, :, :].bitcast(F32), ALU.subtract).then_inc(xT_low, 1)

            def add_attention(b, j):
                dve.wait_ge(attn_done, TB * b + j + 1)
                V.tensor_tensor(x1[:, TB * b + j, :], ps_at[j % 2][:, :], x1[:, TB * b + j, :],
                                ALU.add).then_inc(x1_ready, 1)
                dve.wait_ge(x1_ready, TB * b + j + 1)
                V.bn_stats(stats[:, 1, j, :], x1[:, TB * b + j, :]).then_inc(x1_stats, 1)

            NR, NR_LAST = 27, 25 + 24

            def choose(r, b, lo, n):
                w = slice(lo, lo + n)
                if lo == 0:
                    r.add(V.tensor_copy(cum[:, 0, :], cum[:, TB, :]))
                dve.wait_ge(logits_done, logits_needed(b, lo))
                r.link(V.tensor_copy(rl[:, w, :], choice_bank(b, lo)[:, lo * E:(lo + n) * E].rearrange("p (t e) -> p t e", e=E)))
                src = rl
                for c in range(2):
                    r.link(V.tensor_reduce(top[:, c, w], src[:, w, :], AX_X, ALU.max))
                    r.link(V.tensor_tensor(eq[:, w, :], src[:, w, :], tiles(top[:, c, w], n), ALU.is_equal))
                    r.link(V.tensor_tensor(eq[:, w, :], eq[:, w, :], experts(rev[:, :], n), ALU.mult))
                    r.link(V.tensor_reduce(pick[:, c, w], eq[:, w, :], AX_X, ALU.max))
                    r.link(V.tensor_tensor(oh[:, c, w, :], experts(rev[:, :], n), tiles(pick[:, c, w], n), ALU.is_equal))
                    if c == 0:
                        r.link(V.scalar_tensor_tensor(rl2[:, w, :], oh[:, 0, w, :], -3.0e38, rl[:, w, :], ALU.mult, ALU.add))
                        src = rl2
                r.link(V.tensor_tensor(selb[:, w, :], oh[:, 0, w, :], oh[:, 1, w, :], ALU.add))
                for j in range(lo, lo + n):
                    last = V.tensor_tensor(cum[:, j + 1, :], cum[:, j, :], selb[:, j, :], ALU.add)
                    if j < lo + n - 1:
                        r.link(last)
                last.then_inc(chosen, 1)

            def give_slots(r, b, lo, n):
                w, wb = slice(lo, lo + n), slice(TB * b + lo, TB * b + lo + n)
                for c in range(2):
                    r.add(V.tensor_copy(oh_all[:, c, wb, :], oh[:, c, w, :]))
                r.add(V.tensor_copy(lg_all[:, wb, :], rl[:, w, :]))
                r.add(V.tensor_copy(m_all[:, wb], top[:, 0, w]))
                dve.wait_ge(ranks_done, b + 1 + (lo > 0))
                r.link(V.tensor_tensor(place[:, w, :], choice_bank(b, lo)[:, (TB + lo) * E:(TB + lo + n) * E].rearrange(
                    "p (t e) -> p t e", e=E), experts(cape[:, :], n), ALU.add))
                for c in range(2):
                    r.link(V.tensor_tensor(eq[:, w, :], oh[:, c, w, :], place[:, w, :], ALU.mult))
                    r.link(V.tensor_reduce(slot[:, w, c], eq[:, w, :], AX_X, ALU.add))
                r.add(V.tensor_copy(slot_all[:, wb, :], slot[:, w, :]))
                if b >= 2:
                    dve.wait_ge(scattered[b % 2], 32 * TB * (b // 2))
                V.tensor_copy(slot_i[:, b % 2, w, :], slot[:, w, :]).then_inc(slots_ready, 1)

            def first_layernorm(b):
                c = Chain(dve, ln1_steps, NL1, b)
                ln1_stats(c, b)
                return c

            ctx_maxima(0)
            first = first_layernorm(0)
            c = Chain(dve, quant_steps, NQ0, 0)
            ctx_scales(c, 0)
            ln1_scale(first, 0)
            ctx_to_grid(c, 0, 0)
            first = first_layernorm(1)
            ctx_to_grid(c, 0, 1)
            x_maxima(c, 0)
            scales(c, xmax, xsc, xinv, ACT_EPS, x_scaled)
            ctx_to_grid(c, 0, 2)
            ctx_to_grid(c, 0, 3)
            ln1_scale(first, 1)
            for j in range(TB):
                x_to_grid(c, 0, j)
            c.close()
            low_ctx(0)
            low_x(0, 0)
            low_x(0, 1)
            second = None
            for b in range(B):
                if b + 2 < B:
                    first = first_layernorm(b + 2)
                if b >= 1:
                    ln2_scale(second, b - 1, 1)
                    second.close()
                    r = Chain(dve, choice_steps, NR, b - 1)
                if b + 1 < B:
                    ctx_maxima(b + 1)
                low_x(b, 2)
                low_x(b, 3)
                second = Chain(dve, ln2_steps, NL2, b)
                if b + 1 < B:
                    c = Chain(dve, quant_steps, NQ, b, NQ0)
                    ctx_scales(c, b + 1)
                    x_maxima(c, b + 1)
                    scales(c, xmax, xsc, xinv, ACT_EPS, x_scaled)
                    ctx_magnitude(c, b + 1, 0)
                    ctx_magnitude(c, b + 1, 1)
                if b + 2 < B:
                    ln1_scale(first, b + 2)
                for j in range(HB):
                    if j == 1 and b >= 1 and b + 1 < B:
                        choose(r, b - 1, 0, TB)
                    if b + 1 < B:
                        ctx_magnitude(c, b + 1, HB + j)
                    add_attention(b, j)
                    if b + 1 < B:
                        x_to_grid(c, b + 1, j)
                ln2_aggregate(second, b, 0)
                if b + 1 == B:
                    ln2_scale(second, b, 0)
                    choose(r, b - 1, 0, TB)
                for j in range(HB, TB):
                    add_attention(b, j)
                    if b + 1 < B:
                        x_to_grid(c, b + 1, j)
                    if j == HB:
                        if b + 1 < B:
                            ln2_scale(second, b, 0)
                        else:
                            give_slots(r, b - 1, 0, TB)
                            r.close()
                ln2_aggregate(second, b, 1)
                if b >= 1 and b + 1 < B:
                    give_slots(r, b - 1, 0, TB)
                    r.close()
                if b + 1 < B:
                    c.close()
                    low_ctx(b + 1)
                    low_x(b + 1, 0)
                    low_x(b + 1, 1)
            ln2_scale(second, B - 1, 1)
            second.close()
            V.memset(zero, 0.0).then_inc(zero_ready, 1)
            r = Chain(dve, choice_steps, NR_LAST, 0, NR * (B - 1))
            choose(r, B - 1, 0, HB)
            give_slots(r, B - 1, 0, HB)
            choose(r, B - 1, HB, HB)
            n_rows, n_tiles, upto, base = (count[:, i, :] for i in range(4))
            t = Chain(dve, table_steps, 33, 0)
            dve.wait_ge(counts_done, 1)
            t.link(V.tensor_copy(n_rows, ps_small[:, 0:E]))
            t.link(V.tensor_tensor(tabf[:, T_PAD:T_PAD + E], n_rows, cape[:, :], ALU.add))
            V.tensor_copy(tab[:, T_PAD:T_PAD + E], tabf[:, T_PAD:T_PAD + E]).then_inc(pads_ready, 1)
            give_slots(r, B - 1, HB, HB)
            r.close()

            t.link(V.tensor_scalar(tabf[:, 0:NT], io[:, 0:NT], float(P), None, ALU.mult))
            t.link(V.tensor_tensor(over, n_rows.unsqueeze(2).broadcast_to([P, E, NT]),
                                   tabf[:, 0:NT].unsqueeze(1).broadcast_to([P, E, NT]), ALU.is_gt))
            t.link(V.tensor_reduce(n_tiles, over, AX_X, ALU.add))
            t.link(V.tensor_copy(upto[:, 0:1], n_tiles[:, 0:1]))
            for e in range(1, E):
                t.link(V.tensor_tensor(upto[:, e:e + 1], upto[:, e - 1:e], n_tiles[:, e:e + 1], ALU.add))
            tcol = io[:, 0:NTILE].unsqueeze(2).broadcast_to([P, NTILE, E])
            t.link(V.tensor_tensor(le, tcol, experts(upto, NTILE), ALU.is_ge))
            t.link(V.tensor_tensor(le2, le, experts(alt[:, :], NTILE), ALU.mult))
            t.link(V.tensor_reduce(tabf[:, T_PAR:T_PAR + NTILE], le2[:, :, 0:E - 1], AX_X, ALU.add))
            t.link(V.tensor_reduce(tabf[:, T_WREADY:T_WREADY + NTILE], le[:, :, 0:E - 1], AX_X, ALU.add))
            t.link(V.tensor_tensor(le2, le, experts(n_tiles, NTILE), ALU.mult))
            rowc = tabf[:, T_ROW:T_ROW + NTILE]
            t.link(V.tensor_reduce(rowc, le2[:, :, 0:E - 1], AX_X, ALU.add))
            t.link(V.tensor_tensor(rowc, io[:, 0:NTILE], rowc, ALU.subtract))
            t.link(V.tensor_scalar(rowc, rowc, float(P), None, ALU.mult))
            t.link(V.scalar_tensor_tensor(rowc, tabf[:, T_WREADY:T_WREADY + NTILE], float(CAP), rowc, ALU.mult, ALU.add))
            t.link(V.tensor_scalar(tabf[:, T_WREADY:T_WREADY + NTILE], tabf[:, T_WREADY:T_WREADY + NTILE], 1.0, None, ALU.add))
            idle = le[:, :, E - 1]
            t.link(V.tensor_scalar(le2[:, :, 0], rowc, -1.0, float(ZROW), ALU.mult, ALU.add))
            t.link(V.tensor_tensor(le2[:, :, 0], le2[:, :, 0], idle, ALU.mult))
            t.link(V.tensor_tensor(rowc, rowc, le2[:, :, 0], ALU.add))
            t.link(V.tensor_scalar(tabf[:, T_FREE:T_FREE + E], upto, 1.0, None, ALU.add))
            t.link(V.tensor_tensor(tabf[:, T_LAST:T_LAST + 2], upto[:, E - 1:E].broadcast_to([P, 2]), rev[:, E - 2:E],
                                   ALU.subtract))
            t.link(V.tensor_copy(tabf[:, T_LOW:T_TILES + 1], upto[:, E - 2:E]))
            for lo, n in ((T_PAR, NTILE), (T_WREADY, NTILE), (T_ROW, NTILE)):
                t.link(V.tensor_copy(tab[:, lo:lo + n], tabf[:, lo:lo + n]))
            V.tensor_copy(tab[:, T_FREE:T_END], tabf[:, T_FREE:T_END]).then_inc(table_ready, 1)
            t.link(V.tensor_tensor(base, upto, n_tiles, ALU.subtract))
            t.close()
            m = Chain(dve, mix_steps, 22, 0)
            m.link(V.scalar_tensor_tensor(base, base, float(P), cape[:, :], ALU.mult, ALU.subtract))
            m.link(V.tensor_tensor(ohm, oh_all[:, :, :, :].rearrange("p a t e -> p (a t) e"), experts(base, 2 * NT), ALU.mult))
            m.link(V.tensor_reduce(small[:, 0:2, :].rearrange("p a t -> p (a t)"), ohm, AX_X, ALU.add))
            m.link(V.tensor_tensor(slot_all[:, :, :], slot_all[:, :, :], small[:, 0:2, :].rearrange("p a t -> p t a"), ALU.add))
            first_low = small[:, 4, :]
            m.add(V.tensor_tensor(first_low, slot_all[:, :, 0], slot_all[:, :, 1], ALU.is_lt))
            m.add(V.tensor_tensor(small[:, 0, :], slot_all[:, :, 0], slot_all[:, :, 1], ALU.min))
            m.link(V.tensor_tensor(small[:, 1, :], slot_all[:, :, 0], slot_all[:, :, 1], ALU.max))
            m.link(V.tensor_copy(yrow_i[:, :, :], small[:, 0:2, :].rearrange("p a t -> p t a")))
            V.tensor_tensor(expo, lg_all[:, :, :], m_all[:, :].unsqueeze(2).broadcast_to([P, NT, E]),
                            ALU.subtract).then_inc(exp_in, 1)
            dve.wait_ge(exp_done, 1)
            m.link(V.tensor_reduce(small[:, 2, :], expo2, AX_X, ALU.add))
            m.link(V.reciprocal(small[:, 2, :], small[:, 2, :]))
            m.link(V.tensor_tensor(expo2, expo2, small[:, 2, :].unsqueeze(2).broadcast_to([P, NT, E]), ALU.mult))
            for n in range(2):
                m.link(V.tensor_tensor(expo, expo2, oh_all[:, n, :, :], ALU.mult))
                m.link(V.tensor_reduce(wmix[:, n, :], expo, AX_X, ALU.add))
            m.link(V.tensor_tensor(small[:, 3, :], wmix[:, 0, :], wmix[:, 1, :], ALU.add))
            m.link(V.reciprocal(small[:, 3, :], small[:, 3, :]))
            m.link(V.tensor_tensor(wmix[:, :, :], wmix[:, :, :], small[:, 3, :].unsqueeze(1).broadcast_to([P, 2, NT]),
                                   ALU.mult))
            m.link(V.tensor_scalar(small[:, 5, :], first_low, -1.0, 1.0, ALU.mult, ALU.add))
            m.link(V.tensor_tensor(small[:, 0:2, :], wmix[:, :, :], small[:, 4:6, :], ALU.mult))
            m.link(V.tensor_tensor(small[:, 2:4, :], wmix[:, :, :], small[:, 0:2, :], ALU.subtract))
            m.link(V.tensor_tensor(wmix[:, 0, :], small[:, 0, :], small[:, 1, :], ALU.add))
            V.tensor_tensor(wmix[:, 1, :], small[:, 2, :], small[:, 3, :], ALU.add).then_inc(mix_ready, 1)
            m.close()

            def low_rows(t):
                dve.wait_ge(rT_high, t + 1)
                V.tensor_tensor(rT[:, 1, :, :], ps_rT[:, :].rearrange("p (k c) -> p k c", c=P),
                                rT[:, 0, :, :].bitcast(F32), ALU.subtract).then_inc(rT_low, 1)

            def gate(t):
                dve.wait_ge(up_done, 2 * t + 2)
                dve.wait_ge(silu_done, t + 1)
                V.tensor_tensor(hid, ps_u[:, :], sg, ALU.mult).then_inc(hid_ready, 1)

            def low_hid(t):
                dve.wait_ge(hT_high, t + 1)
                V.tensor_tensor(hT[:, 1, :, :], ps_hT[:, :].rearrange("p (k c) -> p k c", c=P),
                                hT[:, 0, :, :].bitcast(F32), ALU.subtract).then_inc(hT_low, 1)

            low_rows(0)
            gate(0)
            low_rows(1)
            low_hid(0)

            def tile(t):
                gate(t)
                low_rows(t + 1)
                low_hid(t)

            tiles_ = table_value(dve, T_TILES, NFULL)
            with dve.Fori(1, NFULL) as t:
                tile(t)
            with dve.Fori(NFULL, NTILE) as t:
                with dve.If(t < tiles_):
                    tile(t)

            def mix(buf, i, s, which, done):
                xi = x1[:, ds(i, 1), :].rearrange("p a d -> p (a d)")
                V.scalar_tensor_tensor(xi, buf[:, ds(s, 1), :].rearrange("p a d -> p (a d)"), wmix[:, which, ds(i, 1)],
                                       xi, ALU.mult, ALU.add).then_inc(done, 1)

            dve.wait_ge(mix_ready, 1)
            dve.wait_ge(fetched_low, 16 * NT)
            with dve.Fori(0, FLIGHT) as s:
                mix(fetch_buf[0], s, s, 0, low_mixed)
            for i in range(NT):
                dve.wait_ge(low_mixed, min(FLIGHT + i, NT))
                dve.wait_ge(fetched_high[i % FLIGHT], 16 * (i // FLIGHT + 1))
                mix(fetch_buf[i // FLIGHT], i, i % FLIGHT, 1, row_ready)
                if i + FLIGHT < NT:
                    mix(fetch_buf[1], i + FLIGHT, i, 0, low_mixed)

        @block.tensor
        def _(pe):
            def turn_ctx(b):
                for k in range(KC):
                    pe.wait_ge(ctx_ready, TB * (b + 1))
                    if b > 0:
                        pe.wait_ge(xT_low, TB * b)
                    for j in range(TB):
                        last = nc.tensor.transpose(ps_T[k][:, j * P:(j + 1) * P], ctxq[:, j, k * P:(k + 1) * P],
                                                   ident[:, :])
                    last.then_inc(cT_formed, 1)

            def turn_x(b, j):
                pe.wait_ge(xq_ready, TB * b + j + 1)
                pe.wait_ge(cT_low, KC * b + j + 1)
                for k in range(KC):
                    last = nc.tensor.transpose(ps_T[j][:, k * P:(k + 1) * P], xq[:, j, k * P:(k + 1) * P],
                                               ident[:, :])
                last.then_inc(xT_formed, 1)

            def attention(b, j):
                if TB * b + j >= 2:
                    pe.wait_ge(x1_ready, TB * b + j - 1)
                pe.wait_ge(xT_low, TB * b + j + 1)
                n = 0
                for k in range(KC):
                    for xp, cp in ((0, 0), (0, 1), (1, 0)):
                        last = nc.tensor.matmul(ps_at[j % 2][:, :], xT[:, j, xp, k, :], cT[:, cp, k, :],
                                                start=(n == 0), stop=(n == 3 * KC - 1))
                        n += 1
                last.then_inc(attn_done, 1)

            def turn_y2(b, half):
                for j in range(HB * half, HB * half + HB):
                    pe.wait_ge(y2_ready, TB * b + j + 1)
                    for k in range(KC):
                        last = nc.tensor.transpose(turned_in(j)[:, k * P:(k + 1) * P], y2[b % 2][:, j, k * P:(k + 1) * P],
                                                   ident[:, :])
                    last.then_inc(yT_formed, 1)

            def logits(b, half):
                for j in range(HB * half, HB * half + HB):
                    pe.wait_ge(yT_ready, TB * b + j + 1)
                    for k in range(KC):
                        last = nc.tensor.matmul(choice_bank(b, HB * half)[:, j * E:(j + 1) * E], y2T[:, j % 2, k, :], wr[:, k, :],
                                                start=(k == 0), stop=(k == KC - 1))
                if half == 1 or b + 1 == B:
                    last.then_inc(logits_done, 1)

            def router(b, half):
                turn_y2(b, half)
                logits(b, half)

            def ranks(b, lo, n):
                pe.wait_ge(chosen, b + 1 + (lo > 0))
                to = choice_bank(b, lo)[:, (TB + lo) * E:(TB + lo + n) * E]
                nc.tensor.matmul(to, before[:, :], selb[:, lo:lo + n, :].rearrange("p t e -> p (t e)"),
                                 start=True, stop=False)
                nc.tensor.matmul(to, ones[:, :], cum[:, lo:lo + n, :].rearrange("p t e -> p (t e)"),
                                 start=False, stop=True).then_inc(ranks_done, 1)

            pe.wait_ge(masks_ready, 2)
            pe.wait_ge(wr_loaded, 16)
            turn_ctx(0)
            for j in range(TB):
                turn_x(0, j)
            for b in range(B):
                attention(b, 0)
                attention(b, 1)
                if b >= 1:
                    pe.wait_ge(xT_low, TB * (b + 1))
                    router(b - 1, 1)
                attention(b, 2)
                if b + 1 == B:
                    ranks(b - 1, 0, TB)
                attention(b, 3)
                if b >= 1 and b + 1 < B:
                    ranks(b - 1, 0, TB)
                if b + 1 < B:
                    turn_ctx(b + 1)
                    for j in range(TB - 1):
                        turn_x(b + 1, j)
                    if b >= 1:
                        pe.wait_ge(slots_ready, b)
                pe.wait_ge(x1_ready, TB * b + 3)
                router(b, 0)
                if b + 1 < B:
                    turn_x(b + 1, TB - 1)
            turn_y2(B - 1, 1)
            ranks(B - 1, 0, HB)
            logits(B - 1, 1)
            pe.wait_ge(chosen, B + 1)
            nc.tensor.matmul(ps_small[:, 0:E], ones[:, :], cum[:, TB, :], start=True, stop=True).then_inc(counts_done, 1)
            ranks(B - 1, HB, HB)

            def turn_rows(t):
                pe.wait_ge(rows_loaded, 16 * (t + 1))
                for k in range(KC):
                    last = nc.tensor.transpose(ps_rT[:, k * P:(k + 1) * P], rows[:, k * P:(k + 1) * P], ident[:, :])
                return last

            def expert_of(t):
                return pe.value_load(tab[0:1, ds(T_PAR + t, 1)], min_val=0, max_val=1)

            def gate_up(t):
                slot_ = expert_of(t)
                ready = pe.value_load(tab[0:1, ds(T_WREADY + t, 1)], min_val=1, max_val=E)
                pe.wait_ge(w_ready, ready)
                pe.wait_ge(rT_low, t + 1)
                for m, bank in ((0, ps_g), (1, ps_u)):
                    n = 0
                    for k in range(KC):
                        for xp, wp in ((0, 0), (0, 1), (1, 0)):
                            last = nc.tensor.matmul(bank[:, :], rT[:, xp, k, :], wsplit[:, ds(slot_, 1), m, wp, k, :],
                                                    start=(n == 0), stop=(n == 3 * KC - 1))
                            n += 1
                    last.then_inc(up_done, 1)

            def down(t, first=False):
                slot_ = expert_of(t)
                pe.wait_ge(hT_low, t + 1)
                if not first:
                    pe.wait_ge(yt_ready, t)
                n = 0
                for k in range(KC):
                    for hp, wp in ((0, 0), (0, 1), (1, 0)):
                        last = nc.tensor.matmul(ps_y[:, :], hT[:, hp, k, :], wsplit[:, ds(slot_, 1), 2, wp, k, :],
                                                start=(n == 0), stop=(n == 3 * KC - 1))
                        n += 1
                last.then_inc(tiles_done, 1)

            def turn_hid(t):
                pe.wait_ge(hid_ready, t + 1)
                for k in range(KC):
                    last = nc.tensor.transpose(ps_hT[:, k * P:(k + 1) * P], hid[:, k * P:(k + 1) * P], ident[:, :])
                last.then_inc(hT_formed, 1)

            pe.wait_ge(w_ready, 1)
            pe.wait_ge(table_ready, 1)
            for _ in range(WARM_UP):
                nc.tensor.matmul(ps[6][:, :], xT[:, TB - 1, 0, 0, :], wsplit[:, 0, 0, 0, 0, :], start=True, stop=True)
            turn_rows(0).then_inc(rT_formed, 1)
            nc.tensor.matmul(ps_small[:, 0:E], ones[:, :], cum[:, TB, :], start=True, stop=True).then_inc(tiles_done, 1)
            gate_up(0)
            turn_rows(1).then_inc(rT_formed, 1)
            turn_hid(0)
            gate_up(1)
            pe.wait_ge(rT_low, 2)
            turn_rows(2).then_inc(rT_formed, 1)
            down(0, True)
            turn_hid(1)

            def tile(t):
                gate_up(t)
                turn_rows(t + 1).then_inc(rT_formed, 1)
                down(t - 1)
                turn_hid(t)

            tiles_ = table_value(pe, T_TILES, NFULL)
            with pe.Fori(2, NFULL) as t:
                tile(t)
            with pe.Fori(NFULL, NTILE) as t:
                with pe.If(t < tiles_):
                    tile(t)
            down(table_value(pe, T_LAST + 1, NFULL - 1, NTILE - 1))


_INS = ['x', 'ctx_2048', 'L0_ffn_Wr', 'L0_ffn_Wg', 'L0_ffn_Wu', 'L0_ffn_Wd']
_OUTS = [((4, 512, 512), 'float32')]


def kernel(**inputs):
    import numpy as _np
    import concourse.bacc as _bacc
    from concourse import mybir as _mybir
    from concourse.bass_utils import run_bass_kernel_spmd as _run

    nc = _bacc.Bacc("TRN2", target_bir_lowering=False, num_devices=1)
    arrays, args = {}, []
    for name in _INS:
        a = _np.ascontiguousarray(inputs[name])
        arrays[f"in_{name}_dram"] = a
        args.append(nc.dram_tensor(f"in_{name}_dram", a.shape, _mybir.dt.from_np(a.dtype), kind="ExternalInput").ap())
    for i, (shape, dtype) in enumerate(_OUTS):
        dt = _mybir.dt.from_np(_np.dtype(dtype))
        args.append(nc.dram_tensor(f"out_{i}_dram", shape, dt, kind="ExternalOutput").ap())
    xattn_moe(nc, *args)
    r = _run(nc, [arrays], core_ids=[0])
    return r.results[0]["out_0_dram"]
```
